# Optimizing a Trainium2 kernel written in Bass

```python
import numpy as np
import jax
import jax.numpy as jnp

def _softmax(x, axis=-1):
    return jax.nn.softmax(x, axis=axis)

def _gelu(x):
    return jax.nn.gelu(x, approximate=True)

def _silu(x):
    return jax.nn.silu(x)

def _sigmoid(x):
    return jax.nn.sigmoid(x)

def _layernorm(x, axis=-1, eps=1e-05):
    m = jnp.mean(x, axis=axis, keepdims=True)
    v = jnp.var(x, axis=axis, keepdims=True)
    return (x - m) / jnp.sqrt(v + eps)

def _scatter_add(tgt, idx, src, axis=0):
    return tgt.at[idx].add(src)

def _segment_sum(src, seg, n):
    return jax.ops.segment_sum(src, seg, n)
kernel_name = 'mk_macaron_d1_jaxref_r4_b8b996'

def setup_inputs(seed: int=0):
    np.random.seed(seed)
    _w = jnp.asarray

    def _L0_attn_setup():
        import jax, jax.numpy as jnp
        import numpy as np
        D_MODEL = 256
        D_STATE = 128
        D_CONV = 4
        EXPAND = 2
        DT_RANK = max(16, D_MODEL // 16)
        D_INNER = EXPAND * D_MODEL
        BATCH = 4
        SEQ = 1024
        key = jax.random.key(seed)
        ks = jax.random.split(key, 11)
        s = 0.02
        return {'x': jax.random.normal(ks[0], (BATCH, SEQ, D_MODEL), jnp.float32), 'in_proj_w': jax.random.normal(ks[1], (2 * D_INNER, D_MODEL), jnp.float32) * s, 'conv_w': jax.random.normal(ks[2], (D_INNER, 1, D_CONV), jnp.float32) * 0.2, 'conv_b': jax.random.normal(ks[3], (D_INNER,), jnp.float32) * 0.02, 'x_proj_w': jax.random.normal(ks[4], (DT_RANK + 2 * D_STATE, D_INNER), jnp.float32) * s, 'dt_proj_w': jax.random.normal(ks[5], (D_STATE, DT_RANK), jnp.float32), 'dt_proj_b': jax.random.uniform(ks[6], (D_STATE,), jnp.float32, -1.0, 1.0), 'A_log': -jnp.exp(jax.random.normal(ks[7], (D_STATE,), jnp.float32)) - 1.0, 'D': jax.random.normal(ks[8], (D_INNER,), jnp.float32) * 0.02, 'C_proj_w': jax.random.normal(ks[9], (D_INNER, D_STATE), jnp.float32) * s, 'out_proj_w': jax.random.normal(ks[10], (D_MODEL, D_INNER), jnp.float32) * s}
    _L0_attn_in = _L0_attn_setup()

    def _L0_ffn_setup():
        import jax, jax.numpy as jnp
        import numpy as np
        DIM = 256
        HIDDEN = 768
        SCALE = 1.0 / 127.0

        def _dequant(w_int, dtype):
            return w_int.astype(dtype) * jnp.asarray(SCALE, dtype)
        key = jax.random.key(seed)
        k_x, k_g, k_u, k_d = jax.random.split(key, 4)
        x = jax.random.normal(k_x, (4, 512, DIM), dtype=jnp.float32)
        w_gate = jax.random.randint(k_g, (HIDDEN, DIM), -127, 128, dtype=jnp.int32)
        w_up = jax.random.randint(k_u, (HIDDEN, DIM), -127, 128, dtype=jnp.int32)
        w_down = jax.random.randint(k_d, (DIM, HIDDEN), -127, 128, dtype=jnp.int32)
        return {'x': x, 'w_gate': w_gate, 'w_up': w_up, 'w_down': w_down}
    _L0_ffn_in = _L0_ffn_setup()
    _d = {'L0_attn_x': _L0_attn_in['x'], 'L0_attn_in_proj_w': _L0_attn_in['in_proj_w'], 'L0_attn_conv_w': _L0_attn_in['conv_w'], 'L0_attn_conv_b': _L0_attn_in['conv_b'], 'L0_attn_x_proj_w': _L0_attn_in['x_proj_w'], 'L0_attn_dt_proj_w': _L0_attn_in['dt_proj_w'], 'L0_attn_dt_proj_b': _L0_attn_in['dt_proj_b'], 'L0_attn_A_log': _L0_attn_in['A_log'], 'L0_attn_D': _L0_attn_in['D'], 'L0_attn_C_proj_w': _L0_attn_in['C_proj_w'], 'L0_attn_out_proj_w': _L0_attn_in['out_proj_w'], 'L0_ffn_w_gate': _L0_ffn_in['w_gate'], 'L0_ffn_w_up': _L0_ffn_in['w_up'], 'L0_ffn_w_down': _L0_ffn_in['w_down']}
    _x0 = _d['L0_attn_x']
    _d['L0_attn_x'] = jax.random.normal(jax.random.fold_in(jax.random.key(seed), 1), (2, 2048, 256), dtype=_x0.dtype)
    del _x0
    return _d

def reference(L0_attn_x, L0_attn_in_proj_w, L0_attn_conv_w, L0_attn_conv_b, L0_attn_x_proj_w, L0_attn_dt_proj_w, L0_attn_dt_proj_b, L0_attn_A_log, L0_attn_D, L0_attn_C_proj_w, L0_attn_out_proj_w, L0_ffn_w_gate, L0_ffn_w_up, L0_ffn_w_down):

    def _L0_attn_ref(x, in_proj_w, conv_w, conv_b, x_proj_w, dt_proj_w, dt_proj_b, A_log, D, C_proj_w, out_proj_w):
        import jax, jax.numpy as jnp
        import numpy as np
        D_MODEL = 256
        D_STATE = 128
        D_CONV = 4
        EXPAND = 2
        DT_RANK = max(16, D_MODEL // 16)
        D_INNER = EXPAND * D_MODEL
        BATCH = 4
        SEQ = 1024
        B, L, _ = x.shape
        xz = x @ in_proj_w.T
        x_in, z = jnp.split(xz, 2, axis=-1)
        xc = jnp.transpose(x_in, (0, 2, 1))
        xc = jax.lax.conv_general_dilated(xc, conv_w, window_strides=(1,), padding=[(D_CONV - 1, 0)], dimension_numbers=('NCH', 'OIH', 'NCH'), feature_group_count=D_INNER)
        xc = xc + conv_b[None, :, None]
        xc = jnp.transpose(xc, (0, 2, 1))
        ssm = xc @ x_proj_w.T
        dt_r, Bm, _Cm = jnp.split(ssm, [DT_RANK, DT_RANK + D_STATE], axis=-1)
        delta = jax.nn.softplus(dt_r @ dt_proj_w.T + dt_proj_b)
        delta = jnp.clip(delta, 0.001, 0.1)
        A = -jnp.exp(A_log)
        A_bar = jnp.exp(delta * A)
        A_safe = jnp.where(jnp.abs(A) > 1e-08, A, jnp.ones_like(A))
        B_bar = (A_bar - 1.0) / A_safe * Bm

        def step(h, ab_bb):
            ab, bb = ab_bb
            h = ab * h + bb
            return (h, h)
        a_t = jnp.transpose(A_bar, (1, 0, 2))
        b_t = jnp.transpose(B_bar, (1, 0, 2))
        h0 = jnp.zeros((B, D_STATE), x.dtype)
        _, hs = jax.lax.scan(step, h0, (a_t, b_t))
        y = jnp.einsum('lbn,dn->bld', hs, C_proj_w)
        y = y + xc * D
        out = y * jax.nn.silu(z) @ out_proj_w.T
        return out

    def _L0_ffn_ref(x, w_gate, w_up, w_down):
        import jax, jax.numpy as jnp
        import numpy as np
        DIM = 256
        HIDDEN = 768
        SCALE = 1.0 / 127.0

        def _dequant(w_int, dtype):
            return w_int.astype(dtype) * jnp.asarray(SCALE, dtype)
        wg = _dequant(w_gate, x.dtype)
        wu = _dequant(w_up, x.dtype)
        wd = _dequant(w_down, x.dtype)
        gate = jnp.einsum('bsd,hd->bsh', x, wg)
        up = jnp.einsum('bsd,hd->bsh', x, wu)
        h = jax.nn.silu(gate) * up
        return jnp.einsum('bsh,dh->bsd', h, wd)
    x = L0_attn_x
    x = x + 0.5 * _L0_ffn_ref(_layernorm(x, axis=-1), L0_ffn_w_gate, L0_ffn_w_up, L0_ffn_w_down)
    x = x + _L0_attn_ref(_layernorm(x, axis=-1), L0_attn_in_proj_w, L0_attn_conv_w, L0_attn_conv_b, L0_attn_x_proj_w, L0_attn_dt_proj_w, L0_attn_dt_proj_b, L0_attn_A_log, L0_attn_D, L0_attn_C_proj_w, L0_attn_out_proj_w)
    x = x + 0.5 * _L0_ffn_ref(_layernorm(x, axis=-1), L0_ffn_w_gate, L0_ffn_w_up, L0_ffn_w_down)
    return x

_drawn_inputs = setup_inputs


def setup_inputs(seed=0):
    import zlib

    import numpy as np

    out = dict(_drawn_inputs(seed))
    spreads = {}
    factors = {'L0_attn_in_proj_w': 8.0,
     'L0_attn_conv_w': 8.0,
     'L0_attn_conv_b': 8.0,
     'L0_attn_x_proj_w': 8.0,
     'L0_attn_dt_proj_w': 8.0,
     'L0_attn_dt_proj_b': 21.794,
     'L0_attn_A_log': 8.0,
     'L0_attn_D': 64.0,
     'L0_attn_C_proj_w': 8.0,
     'L0_attn_out_proj_w': 8.0}
    for name, (base, spread) in spreads.items():
        noise = np.random.default_rng([zlib.crc32(name.encode()), seed]).standard_normal(out[name].shape)
        drawn = base * np.exp(spread * noise) if base else spread * noise
        out[name] = jnp.asarray(drawn.astype(out[name].dtype))
    for name, factor in factors.items():
        out[name] = (out[name] * factor).astype(out[name].dtype)
    return out
```

```python
from contextlib import ExitStack

import concourse.bass as bass
from concourse import mybir

P = 128
B, L, D = 2, 2048, 256
TILE = 512
NB = TILE // P
STEPS = L // TILE
KD = D // P
HID = 768
HC = HID // P
INNER = 512
IC = INNER // P
N = 128
RANK = 16
TAPS = 4
EPS = 1e-5
QUANT = 1.0 / 127.0
XS = 256.0
SMALL = 0.0625

F32, F16, BF16, I32 = mybir.dt.float32, mybir.dt.float16, mybir.dt.bfloat16, mybir.dt.int32
U32 = mybir.dt.uint32
ALU = mybir.AluOpType
ACT = mybir.ActivationFunctionType
AX = mybir.AxisListType

NORM_A, NORM_B, NORM_C = 0, 1, 2

ORDER = [("T", NORM_A, 0), ("T", NORM_A, 1), ("gu", 0, 0), ("gu", 0, 1), ("dn", 0, 0), ("dn", 0, 1),
         ("T", NORM_B, 0), ("ix", 0), ("T", NORM_B, 1), ("iz", 0), ("ix", 1), ("xp", 0), ("iz", 1),
         ("xp", 1), ("cp", 0), ("op", 0), ("cp", 1), ("op", 1),
         ("T", NORM_C, 0), ("gu", 1, 0), ("T", NORM_C, 1), ("gu", 1, 1), ("dn", 1, 0), ("dn", 1, 1)]
RING = 4
LEAD = 1
SSM_STEPS = 8


def ring_table():
    table, at = {}, 0
    for stage in ORDER:
        uses = {"gu": 2 * HC, "ix": IC, "iz": IC, "xp": 2, "cp": IC}.get(stage[0], 0)
        for u in range(uses):
            table[stage + (u,)] = (at % RING, at // RING)
            at += 1
    assert at % RING == 0
    return table, at // RING


def macaron(nc, x, in_w, conv_w, conv_b, xp_w, dt_w, dt_b, a_log, d_skip, c_w, out_w, wg, wu, wd, out):
    Q, QUSES = ring_table()
    HELD = {where: key for key, where in Q.items()}
    with ExitStack() as ctx:
        def sb(name, shape, dt=F32):
            return ctx.enter_context(nc.sbuf_tensor(name, shape, dt))

        def psum(name):
            return ctx.enter_context(nc.psum_tensor(name, [P, 512], F32))

        def sem(name):
            return ctx.enter_context(nc.semaphore(name))

        S2 = range(B)
        X = [sb(f"x{s}", [P, NB, D]) for s in S2]
        XPRE = [sb(f"xpre{s}", [P, NB, D]) for s in S2]
        XN = [sb(f"xn{s}", [P, NB, D]) for s in S2]
        XH = [sb(f"xh{s}", [P, KD, TILE], F16) for s in S2]
        XL = [sb(f"xl{s}", [P, KD, TILE], F16) for s in S2]
        HH = [sb(f"hh{s}", [P, HC, TILE], F16) for s in S2]
        HL = [sb(f"hl{s}", [P, HC, TILE], F16) for s in S2]
        XI = [sb(f"xi{s}", [P, IC, TILE + 4]) for s in S2]
        XC = [sb(f"xc{s}", [P, IC, TILE]) for s in S2]
        SZ = [sb(f"sz{s}", [P, IC, TILE]) for s in S2]
        YU = [sb(f"yu{s}", [P, IC, TILE]) for s in S2]
        PC = [sb(f"pc{s}", [P, TILE]) for s in S2]
        SP = [sb(f"sp{s}", [P, TILE]) for s in S2]
        DL = [sb(f"dl{s}", [P, TILE]) for s in S2]
        EX = [sb(f"ex{s}", [P, TILE]) for s in S2]
        BM = [sb(f"bm{s}", [P, TILE]) for s in S2]
        HS = [sb(f"hs{s}", [P, TILE]) for s in S2]
        CARRY = sb("carry", [P, B])
        SG = sb("sg", [P, 2, TILE])
        H = sb("h", [P, 3, TILE])
        EP = sb("ep", [P, TILE])
        DA = sb("da", [P, TILE])
        RE = sb("re", [P, TILE])
        SER = sb("ser", [P, TILE])
        AB = sb("ab", [P, TILE])
        BB = sb("bb", [P, TILE])
        ST = sb("st", [P, NB, 6])
        MV = sb("mv", [P, NB, 3])
        MN = sb("mn", [P, NB])
        VO = sb("vo", [P, NB])
        VI = sb("vi", [P, NB])
        RS = sb("rs", [P, NB])
        VE = sb("ve", [P, NB])
        NEGH = sb("negh", [P, 2 * HC])
        IDN = sb("idn", [P, P])
        WG = sb("wg", [P, KD, HID], BF16)
        WU = sb("wu", [P, KD, HID], BF16)
        WD = sb("wd", [P, HC, D], BF16)
        WIH = sb("wih", [P, KD, 2 * INNER], F16)
        WIL = sb("wil", [P, KD, 2 * INNER], F16)
        WXB = sb("wxb", [P, IC, N])
        WXD = sb("wxd", [P, IC, N])
        WC = sb("wc", [P, INNER])
        WO = sb("wo", [P, IC, D])
        CW = sb("cw", [P, IC, TAPS])
        CB = sb("cb", [P, IC])
        DS = sb("ds", [P, IC])
        DTB = sb("dtb", [P, 1])
        AL = sb("al", [P, 1])
        A = sb("a", [P, 1])
        NM = sb("nm", [P, 1], I32)
        IA = sb("ia", [P, 1])
        ONE = sb("one", [P, 1])
        NSM = sb("nsm", [P, 1])
        NA = sb("na", [P, 1])
        SSQ = sb("ssq", [P, 2, HC])
        HSC = sb("hsc", [P, HC])
        HSM = sb("hsm", [P, HC])
        HSI = sb("hsi", [P, HC])
        RMX = sb("rmx", [P, 2 * IC])
        RSC = sb("rsc", [P, 2 * IC])
        RIV = sb("riv", [P, 2 * IC])
        DTN = sb("dtn", [P, RANK])
        XPD = sb("xpd", [RANK, INNER])
        DTT = sb("dtt", [RANK, N])
        NGI = HH[0][:, :, :].bitcast(I32).rearrange("p c (u f) -> p (c u) f", f=D)
        NUI = HL[0][:, :, :].bitcast(I32).rearrange("p c (u f) -> p (c u) f", f=D)
        NDI = HH[1][:, :, :].bitcast(I32).rearrange("p c t -> p (c t)").rearrange("p (a h) -> p a h", h=HID)
        NG = SZ[0][:, 0:3, :].rearrange("p c (u f) -> p (c u) f", f=D)
        NU = SZ[1][:, 0:3, :].rearrange("p c (u f) -> p (c u) f", f=D)
        ND = YU[0][:, 0:3, :].rearrange("p c t -> p (c t)").rearrange("p (a h) -> p a h", h=HID)
        SQG = XI[0][:, 0:3, 0:512].rearrange("p c (u f) -> p c u f", f=D)
        SQU = XI[1][:, 0:3, 0:512].rearrange("p c (u f) -> p c u f", f=D)
        NI = XC[0][:, :, :].rearrange("p c (u f) -> p (c u) f", f=D)
        NIS = XC[1][:, :, :].rearrange("p c (u f) -> p (c u) f", f=D)
        NX = YU[1][:, 0, :]
        NC = YU[1][:, 1, :].rearrange("p (m n) -> p m n", n=N)
        NO = YU[1][:, 2:4, :]

        q = [psum(f"q{j}") for j in range(RING)]
        tp = [psum(f"tp{j}") for j in range(KD)]
        dp = [psum(f"dp{j}") for j in range(2)]

        ld_x = [sem(f"ld_x{s}") for s in S2]
        ld = {n: sem("ld_" + n) for n in ("g", "u", "d", "i", "x", "c", "o", "dt", "small")}
        st_y = [sem(f"st_y{s}") for s in S2]
        idn_zero, idn_ready = sem("idn_zero"), sem("idn_ready")
        cast_g, cast_u, cast_d = sem("cast_g"), sem("cast_u"), sem("cast_d")
        sq_u = sem("sq_u")
        in_scaled = sem("in_scaled")
        w_full = [sem(f"w_full{j}") for j in range(RING)]
        w_hi = sem("w_hi")
        w_free = [sem(f"w_free{j}") for j in range(RING)]
        dt_turned = sem("dt_turned")
        dtt_ready = sem("dtt_ready")
        small = sem("small")
        exp_a = sem("exp_a")
        const_ready = sem("const_ready")
        zeroed = sem("zeroed")
        res_done = sem("res_done")
        ln_step, rs_ready = sem("ln_step"), sem("rs_ready")
        negh_ready, ssq_root = sem("negh_ready"), sem("ssq_root")
        xn_ready = sem("xn_ready")
        t_full = [sem(f"t_full{j}") for j in range(KD)]
        t_hi = [sem(f"t_hi{j}") for j in range(KD)]
        t_lo = [sem(f"t_lo{j}") for j in range(KD)]
        q_full = [sem(f"q_full{j}") for j in range(RING)]
        d_full = [sem(f"d_full{j}") for j in range(2)]
        sg_ready, h_ready, hh_ready, hl_ready = sem("sg_ready"), sem("h_ready"), sem("hh_ready"), sem("hl_ready")
        xi_ready, xi_free, conv_step = sem("xi_ready"), sem("xi_free"), sem("conv_step")
        sz_ready, yu_half, yu_ready = sem("sz_ready"), sem("yu_half"), sem("yu_ready")
        pc_ready, ep_ready, sp_ready = sem("pc_ready"), sem("ep_ready"), sem("sp_ready")
        ex_ready, bm_ready = sem("ex_ready"), sem("bm_ready")
        ssm_step, hs_ready, carried = sem("ssm_step"), sem("hs_ready"), sem("carried")

        def xrows(s, t):
            return x[s, bass.ds(t * TILE, TILE), :].rearrange("(b p) d -> p b d", p=P)

        def orows(s, t):
            return out[s, bass.ds(t * TILE, TILE), :].rearrange("(b p) d -> p b d", p=P)

        FILLS = ([("g", j) for j in range(3)] + [("u", j) for j in range(3)] + [("d", j) for j in range(3)]
                 + [("i", j) for j in range(4)] + [("x", 0), ("dt", 0), ("c", 0), ("o", 0), ("o", 1)])
        FILL_AT = {f: (n % RING, n // RING) for n, f in enumerate(FILLS)}
        FILLS_OF = [sum(1 for n in range(len(FILLS)) if n % RING == j) for j in range(RING)]

        block = ctx.enter_context(nc.Block())

        @block.sync
        def _(sp):
            for free in st_y:
                sp.sem_inc(free, LEAD)
            for s in S2:
                sp.dma_start(XPRE[s][:, :, :], xrows(s, 0)).then_inc(ld_x[s], 16)
            sp.dma_start(NUI, wu.rearrange("(c p) f -> p c f", p=P)).then_inc(ld["u"], 16)
            sp.dma_start(NI, in_w.rearrange("(c p) f -> p c f", p=P)).then_inc(ld["i"], 16)
            sp.dma_start(NX, xp_w[RANK:RANK + N, :]).then_inc(ld["x"], 16)
            sp.dma_start(XPD[:, :], xp_w[0:RANK, :]).then_inc(ld["dt"], 16)
            sp.dma_start(NC, c_w.rearrange("(m p) n -> p m n", p=P)).then_inc(ld["c"], 16)
            sp.dma_start(NO, out_w.rearrange("(a p) i -> p a i", p=P)).then_inc(ld["o"], 16)

            def load_next(i):
                for s in S2:
                    sp.wait_ge(res_done, LEAD + 12 * i + 2 * s + 2)
                    sp.dma_start(XPRE[s][:, :, :], xrows(s, i + 1)).then_inc(ld_x[s], 16)

            def store(i):
                for s in S2:
                    sp.wait_ge(res_done, LEAD + 12 * i + 4 * NORM_C + 2 * s + 2)
                    sp.dma_start(orows(s, i), X[s][:, :, :]).then_inc(st_y[s], 16)

            with sp.Fori(0, STEPS - 1) as i:
                load_next(i)
                store(i)
            store(STEPS - 1)
            for s in S2:
                sp.wait_ge(st_y[s], LEAD + 16 * STEPS)





        @block.gpsimd
        def _(pool):
            for free in (hl_ready, yu_ready):
                pool.sem_inc(free, LEAD)
            pool.memset(IDN[:, :], 0.0).then_inc(idn_zero, 1)
            pool.wait_ge(idn_zero, 1)
            pool.affine_select(out=IDN[:, :], in_=IDN[:, :], compare_op=ALU.not_equal, fill=1.0, base=0,
                               pattern=[[-1, P]], channel_multiplier=1).then_inc(idn_ready, 1)
            pool.memset(NEGH[:, :], -0.5).then_inc(negh_ready, 1)

            def root(i, k, s):
                u = 2 * k + s
                pool.wait_ge(ln_step, 24 * i + 4 * u + 4)
                pool.tensor_tensor(RS[:, :], VE[:, :], NEGH[:, 0:NB], ALU.pow).then_inc(rs_ready, 1)

            pool.wait_ge(negh_ready, 1)
            pool.wait_ge(cast_u, 1)
            pool.tensor_tensor(SQU, NU.rearrange("p (a u) f -> p a u f", u=2),
                               NU.rearrange("p (a u) f -> p a u f", u=2), ALU.mult).then_inc(sq_u, 1)
            pool.wait_ge(ld["d"], 16)
            pool.tensor_copy(ND, NDI).then_inc(cast_d, 1)
            root(0, NORM_A, 0)
            root(0, NORM_A, 1)
            pool.wait_ge(small, 4)
            pool.tensor_tensor(SSQ[:, :, :].rearrange("p a c -> p (a c)"),
                               SSQ[:, :, :].rearrange("p a c -> p (a c)"), NEGH[:, :], ALU.pow)\
                .then_inc(ssq_root, 1)

            def hidden_low(i, ffn, s):
                for c in range(HC):
                    n = HC * (2 * ffn + s) + c
                    pool.wait_ge(hh_ready, 24 * i + n + 1)
                    pool.tensor_tensor(HL[s][:, c, :], H[:, n % 3, :], HH[s][:, c, :], ALU.subtract)\
                        .then_inc(hl_ready, 1)

            def gate_y(i, s):
                for m in range(IC):
                    pool.wait_ge(sz_ready, 2 * IC * i + IC * s + m + 1)
                    pool.wait_ge(yu_half, 2 * IC * i + IC * s + m + 1)
                    pool.tensor_tensor(YU[s][:, m, :], YU[s][:, m, :], SZ[s][:, m, :], ALU.mult)\
                        .then_inc(yu_ready, 1)

            def body(i):
                hidden_low(i, 0, 0)
                hidden_low(i, 0, 1)
                root(i, NORM_B, 0)
                root(i, NORM_B, 1)
                gate_y(i, 0)
                root(i, NORM_C, 0)
                gate_y(i, 1)
                root(i, NORM_C, 1)
                hidden_low(i, 1, 0)

            with pool.Fori(0, STEPS - 1) as i:
                body(i)
                root(i + 1, NORM_A, 0)
                root(i + 1, NORM_A, 1)
                hidden_low(i, 1, 1)
            body(STEPS - 1)
            hidden_low(STEPS - 1, 1, 1)

        @block.scalar
        def _(act):
            act.sem_inc(sg_ready, LEAD)
            act.dma_start(NGI, wg.rearrange("(c p) f -> p c f", p=P)).then_inc(ld["g"], 16)
            act.dma_start(NDI, wd.rearrange("(a p) h -> p a h", p=P)).then_inc(ld["d"], 16)
            act.dma_start(DTN[:, :], dt_w).then_inc(ld["dt"], 16)
            act.dma_start(CW[:, :, :], conv_w.rearrange("(m p) o k -> p m (o k)", p=P)).then_inc(ld["small"], 16)
            act.dma_start(CB[:, :], conv_b.rearrange("(m p) -> p m", p=P), allow_slow_non_contiguous=True).then_inc(ld["small"], 16)
            act.dma_start(DS[:, :], d_skip.rearrange("(m p) -> p m", p=P), allow_slow_non_contiguous=True).then_inc(ld["small"], 16)
            act.dma_start(DTB[:, :], dt_b.rearrange("(p o) -> p o", o=1)).then_inc(ld["small"], 16)
            act.dma_start(AL[:, :], a_log.rearrange("(p o) -> p o", o=1)).then_inc(ld["small"], 16)
            act.wait_ge(ld["g"], 16)
            act.activation(NG, NGI, ACT.Copy).then_inc(cast_g, 1)
            act.wait_ge(ld["small"], 80)
            act.activation(EP[:, 0:1], AL[:, :], ACT.Exp).then_inc(exp_a, 1)

            def fill(f, dst, src, scale=None):
                j, k = FILL_AT[f]
                act.wait_ge(w_full[j], k + 1)
                return act.activation(dst, src, ACT.Copy, **({} if scale is None else {"scale": scale}))

            for j in range(3):
                fill(("g", j), WG[:, :, 2 * P * j:2 * P * (j + 1)],
                     q[FILL_AT[("g", j)][0]][:, :].rearrange("p (k h) -> p k h", k=KD))\
                    .then_inc(w_free[FILL_AT[("g", j)][0]], 1)
            for j in range(3):
                fill(("u", j), WU[:, :, 2 * P * j:2 * P * (j + 1)],
                     q[FILL_AT[("u", j)][0]][:, :].rearrange("p (k h) -> p k h", k=KD))\
                    .then_inc(w_free[FILL_AT[("u", j)][0]], 1)
            act.wait_ge(const_ready, 1)
            for j in range(3):
                b = FILL_AT[("d", j)][0]
                fill(("d", j), WD[:, 2 * j, :], q[b][:, 0:D], HSI[:, 2 * j:2 * j + 1])
                act.activation(WD[:, 2 * j + 1, :], q[b][:, D:2 * D], ACT.Copy,
                               scale=HSI[:, 2 * j + 1:2 * j + 2]).then_inc(w_free[b], 1)
            for j in range(4):
                kc, half = j // 2, j % 2
                b = FILL_AT[("i", j)][0]
                fill(("i", j), WIH[:, kc, 512 * half:512 * (half + 1)], q[b][:, :]).then_inc(w_hi, 1)
            fill(("x", 0), WXB[:, :, :].rearrange("p k n -> p (k n)"), q[FILL_AT[("x", 0)][0]][:, :])\
                .then_inc(w_free[FILL_AT[("x", 0)][0]], 1)
            act.wait_ge(dt_turned, 1)
            act.activation(DTT[:, :], tp[0][0:RANK, 0:N], ACT.Copy).then_inc(dtt_ready, 1)
            fill(("dt", 0), WXD[:, :, :].rearrange("p k n -> p (k n)"), q[FILL_AT[("dt", 0)][0]][:, :])\
                .then_inc(w_free[FILL_AT[("dt", 0)][0]], 1)
            fill(("c", 0), WC[:, :], q[FILL_AT[("c", 0)][0]][:, :]).then_inc(w_free[FILL_AT[("c", 0)][0]], 1)
            for j in range(2):
                b = FILL_AT[("o", j)][0]
                fill(("o", j), WO[:, 2 * j:2 * j + 2, :], q[b][:, :].rearrange("p (k h) -> p k h", k=2))\
                    .then_inc(w_free[b], 1)
            act.wait_ge(const_ready, 2)
            act.wait_ge(zeroed, 2)

            def norm_hi(i, k, s):
                u = 2 * k + s
                for kc in range(KD):
                    act.wait_ge(t_full[kc], 6 * i + u + 1)
                    act.activation(XH[s][:, kc, :], tp[kc][:, :], ACT.Copy, scale=XS).then_inc(t_hi[kc], 1)

            def hidden(i, ffn, s):
                for c in range(HC + 1):
                    n = HC * (2 * ffn + s) + c
                    if c < HC:
                        bank, use = Q[("gu", ffn, s, 2 * c)]
                        act.wait_ge(q_full[bank], QUSES * i + use + 1)
                        act.wait_ge(h_ready, LEAD + 24 * i + max(n - 1, 0))
                        act.activation(SG[:, n % 2, :], q[bank][:, :], ACT.Silu, scale=QUANT / XS).then_inc(sg_ready, 1)
                    if c > 0:
                        act.wait_ge(h_ready, LEAD + 24 * i + n)
                        act.activation(HH[s][:, c - 1, :], H[:, (n - 1) % 3, :], ACT.Copy).then_inc(hh_ready, 1)

            def conv_in(i, s):
                act.wait_ge(xi_free, LEAD + 2 * i + (1 if s else 0))
                for m in range(IC):
                    bank, use = Q[("ix", s, m)]
                    act.wait_ge(q_full[bank], QUSES * i + use + 1)
                    act.activation(XI[s][:, m, 3:3 + TILE], q[bank][:, :], ACT.Copy, scale=RIV[:, m:m + 1])\
                        .then_inc(xi_ready, 1)

            def silu_z(i, s):
                act.wait_ge(yu_ready, LEAD + 2 * IC * i)
                for m in range(IC):
                    bank, use = Q[("iz", s, m)]
                    act.wait_ge(q_full[bank], QUSES * i + use + 1)
                    act.activation(SZ[s][:, m, :], q[bank][:, :], ACT.Silu, scale=RIV[:, IC + m:IC + m + 1])\
                        .then_inc(sz_ready, 1)

            def state_in(i, s):
                bank, use = Q[("xp", s, 0)]
                act.wait_ge(q_full[bank], QUSES * i + use + 1)
                act.activation(BM[s][:, :], q[bank][:, :], ACT.Copy, scale=IA[:, 0:1])\
                    .then_inc(bm_ready, 1)
                act.wait_ge(pc_ready, 2 * i + s + 1)
                act.activation(EP[:, :], PC[s][:, :], ACT.Exp).then_inc(ep_ready, 1)
                act.wait_ge(ep_ready, 2 * i + s + 1)
                act.activation(SP[s][:, :], EP[:, :], ACT.Ln, bias=ONE[:, 0:1]).then_inc(sp_ready, 1)
                act.wait_ge(ssm_step, SSM_STEPS * (2 * i + s) + 1)
                act.activation(RE[:, :], DL[s][:, :], ACT.Relu, bias=NSM[:, 0:1], scale=NA[:, 0:1])\
                    .then_inc(ex_ready, 1)
                act.wait_ge(ex_ready, 4 * i + 2 * s + 1)
                act.activation(EX[s][:, :], RE[:, :], ACT.Exp, scale=-1.0).then_inc(ex_ready, 1)

            with act.Fori(0, STEPS) as i:
                norm_hi(i, NORM_A, 0)
                norm_hi(i, NORM_A, 1)
                hidden(i, 0, 0)
                hidden(i, 0, 1)
                norm_hi(i, NORM_B, 0)
                conv_in(i, 0)
                norm_hi(i, NORM_B, 1)
                silu_z(i, 0)
                conv_in(i, 1)
                state_in(i, 0)
                silu_z(i, 1)
                state_in(i, 1)
                norm_hi(i, NORM_C, 0)
                hidden(i, 1, 0)
                norm_hi(i, NORM_C, 1)
                hidden(i, 1, 1)

        @block.vector
        def _(dve):
            for free in (h_ready, res_done, xi_free, carried, *t_lo):
                dve.sem_inc(free, LEAD)
            dve.memset(CARRY[:, :], 0.0).then_inc(zeroed, 1)
            dve.memset(NSM[:, :], -SMALL)
            dve.memset(ONE[:, :], 1.0).then_inc(zeroed, 1)

            def norm_stats(i, k, s):
                u = 4 * (2 * k + s)
                if k == NORM_A:
                    dve.wait_ge(ld_x[s], 16 * i + 16)
                else:
                    dve.wait_ge(res_done, LEAD + 12 * i + 4 * k + 2 * s - 2)
                src = XPRE[s] if k == NORM_A else X[s]
                for b in range(NB):
                    ins = dve.bn_stats(ST[:, b, :], src[:, b, :])
                ins.then_inc(ln_step, 1)
                dve.wait_ge(ln_step, 24 * i + u + 1)
                dve.tensor_tensor(MV[:, :, 0], ST[:, :, 1], ST[:, :, 4], ALU.add)
                dve.tensor_tensor(MV[:, :, 1], ST[:, :, 1], ST[:, :, 4], ALU.subtract)
                dve.tensor_tensor(MV[:, :, 2], ST[:, :, 2], ST[:, :, 5], ALU.add).then_inc(ln_step, 1)
                dve.wait_ge(ln_step, 24 * i + u + 2)
                dve.tensor_scalar(MN[:, :], MV[:, :, 0], 0.5, None, ALU.mult)
                dve.scalar_tensor_tensor(out=VO[:, :], in0=MV[:, :, 1], scalar=0.25, in1=MV[:, :, 1],
                                         op0=ALU.mult, op1=ALU.mult)
                dve.tensor_scalar(VI[:, :], MV[:, :, 2], 1.0 / D, EPS, ALU.mult, ALU.add).then_inc(ln_step, 1)
                dve.wait_ge(ln_step, 24 * i + u + 3)
                dve.tensor_tensor(VE[:, :], VO[:, :], VI[:, :], ALU.add).then_inc(ln_step, 1)
                dve.wait_ge(rs_ready, 6 * i + 2 * k + s + 1)
                if k != NORM_A:
                    dve.wait_ge(t_full[KD - 1], 6 * i + 2 * k + s - 1)
                for b in range(NB):
                    ins = dve.tensor_scalar(XN[s][:, b, :], src[:, b, :], MN[:, b:b + 1], RS[:, b:b + 1],
                                            ALU.subtract, ALU.mult)
                ins.then_inc(xn_ready, 1)

            def norm_lo(i, k, s):
                u = 2 * k + s
                for kc in range(KD):
                    dve.wait_ge(t_hi[kc], 6 * i + u + 1)
                    dve.scalar_tensor_tensor(out=XL[s][:, kc, :], in0=tp[kc][:, :], scalar=XS,
                                             in1=XH[s][:, kc, :], op0=ALU.mult, op1=ALU.subtract)\
                        .then_inc(t_lo[kc], 1)

            def hidden(i, ffn, s):
                for c in range(HC):
                    n = HC * (2 * ffn + s) + c
                    bank, use = Q[("gu", ffn, s, 2 * c + 1)]
                    dve.wait_ge(q_full[bank], QUSES * i + use + 1)
                    dve.wait_ge(sg_ready, LEAD + 24 * i + n + 1)
                    dve.wait_ge(hl_ready, LEAD + 24 * i + max(n - 2, 0))
                    dve.scalar_tensor_tensor(out=H[:, n % 3, :], in0=SG[:, n % 2, :], scalar=HSM[:, c:c + 1],
                                             in1=q[bank][:, :], op0=ALU.mult, op1=ALU.mult)\
                        .then_inc(h_ready, 1)

            def residual(i, k, s):
                if k == NORM_A:
                    dve.wait_ge(st_y[s], LEAD + 16 * i)
                for j in range(2):
                    dve.wait_ge(d_full[j], 6 * i + 2 * k + s + 1)
                    src = XPRE[s] if k == NORM_A else X[s]
                    dve.scalar_tensor_tensor(
                        out=X[s][:, 2 * j:2 * j + 2, :], in0=dp[j][:, :].rearrange("p (b d) -> p b d", d=D),
                        scalar=1.0 if k == NORM_B else 0.5 * QUANT, in1=src[:, 2 * j:2 * j + 2, :],
                        op0=ALU.mult, op1=ALU.add).then_inc(res_done, 1)

            def conv(i, s):
                for m in range(IC):
                    n = IC * s + m
                    dve.wait_ge(xi_ready, 2 * IC * i + n + 1)
                    dve.tensor_scalar(XC[s][:, m, :], XI[s][:, m, 3:3 + TILE], CW[:, m, 3:4], CB[:, m:m + 1],
                                      ALU.mult, ALU.add).then_inc(conv_step, 1)
                    for k in (2, 1, 0):
                        dve.wait_ge(conv_step, TAPS * (2 * IC * i + n) + TAPS - 1 - k)
                        dve.scalar_tensor_tensor(out=XC[s][:, m, :], in0=XI[s][:, m, k:k + TILE],
                                                       scalar=CW[:, m, k:k + 1], in1=XC[s][:, m, :],
                                                       op0=ALU.mult, op1=ALU.add).then_inc(conv_step, 1)
                dve.wait_ge(conv_step, TAPS * (2 * IC * i + IC * (s + 1)))
                dve.tensor_copy(XI[s][:, :, 0:3], XI[s][:, :, TILE:TILE + 3]).then_inc(xi_free, 1)

            def delta(i, s):
                bank, use = Q[("xp", s, 1)]
                dve.wait_ge(q_full[bank], QUSES * i + use + 1)
                dve.tensor_scalar(PC[s][:, :], q[bank][:, :], DTB[:, 0:1], 0.0, ALU.add, ALU.min)\
                    .then_inc(pc_ready, 1)

            def scan(i, s):
                at = SSM_STEPS * (2 * i + s)
                dve.wait_ge(sp_ready, 2 * i + s + 1)
                dve.tensor_scalar(DL[s][:, :], SP[s][:, :], 0.001, 0.1, ALU.max, ALU.min).then_inc(ssm_step, 1)
                dve.wait_ge(ssm_step, at + 1)
                dve.tensor_scalar(DA[:, :], DL[s][:, :], A[:, 0:1], -SMALL, ALU.mult, ALU.max).then_inc(ssm_step, 1)
                dve.wait_ge(ssm_step, at + 2)
                dve.scalar_tensor_tensor(out=SER[:, :], in0=DA[:, :], scalar=4.0, in1=DA[:, :],
                                         op0=ALU.add, op1=ALU.mult).then_inc(ssm_step, 1)
                dve.wait_ge(ssm_step, at + 3)
                dve.scalar_tensor_tensor(out=SER[:, :], in0=SER[:, :], scalar=12.0, in1=DA[:, :],
                                         op0=ALU.add, op1=ALU.mult).then_inc(ssm_step, 1)
                dve.wait_ge(ssm_step, at + 4)
                dve.scalar_tensor_tensor(out=SER[:, :], in0=SER[:, :], scalar=24.0, in1=DA[:, :],
                                         op0=ALU.add, op1=ALU.mult).then_inc(ssm_step, 1)
                dve.wait_ge(ssm_step, at + 5)
                dve.tensor_scalar(SER[:, :], SER[:, :], 1.0 / 24.0, 1.0, ALU.mult, ALU.add).then_inc(ssm_step, 1)
                dve.wait_ge(ssm_step, at + 6)
                dve.wait_ge(ex_ready, 4 * i + 2 * s + 2)
                dve.tensor_tensor(AB[:, :], SER[:, :], EX[s][:, :], ALU.mult).then_inc(ssm_step, 1)
                dve.wait_ge(ssm_step, at + 7)
                dve.wait_ge(bm_ready, 2 * i + s + 1)
                dve.scalar_tensor_tensor(out=BB[:, :], in0=AB[:, :], scalar=-1.0, in1=BM[s][:, :],
                                         op0=ALU.add, op1=ALU.mult).then_inc(ssm_step, 1)
                dve.wait_ge(ssm_step, at + 8)
                dve.wait_ge(carried, LEAD + 2 * i + s)
                dve.tensor_tensor_scan(HS[s][:, :], AB[:, :], BB[:, :], CARRY[:, s:s + 1],
                                       ALU.mult, ALU.add).then_inc(hs_ready, 1)
                dve.wait_ge(hs_ready, 2 * i + s + 1)
                dve.tensor_copy(CARRY[:, s:s + 1], HS[s][:, TILE - 1:TILE]).then_inc(carried, 1)

            def skip_y(i, s):
                for m in range(IC):
                    bank, use = Q[("cp", s, m)]
                    dve.wait_ge(q_full[bank], QUSES * i + use + 1)
                    dve.scalar_tensor_tensor(out=YU[s][:, m, :], in0=XC[s][:, m, :], scalar=DS[:, m:m + 1],
                                             in1=q[bank][:, :], op0=ALU.mult, op1=ALU.add)\
                        .then_inc(yu_half, 1)

            dve.wait_ge(ld["u"], 16)
            dve.tensor_copy(NU, NUI).then_inc(cast_u, 1)
            norm_stats(0, NORM_A, 0)
            norm_stats(0, NORM_A, 1)
            step = [0]

            def chain(ins):
                step[0] += 1
                ins.then_inc(small, 1)
                dve.wait_ge(small, step[0])

            dve.wait_ge(cast_g, 1)
            chain(dve.tensor_tensor(SQG, NG.rearrange("p (a u) f -> p a u f", u=2),
                                    NG.rearrange("p (a u) f -> p a u f", u=2), ALU.mult))
            chain(dve.tensor_reduce(SSQ[:, 0, :].rearrange("p (a u) -> p a u", u=2), SQG, AX.X, ALU.add))
            dve.wait_ge(sq_u, 1)
            chain(dve.tensor_reduce(SSQ[:, 1, :].rearrange("p (a u) -> p a u", u=2), SQU, AX.X, ALU.add))
            chain(dve.tensor_scalar(SSQ[:, :, :], SSQ[:, :, :], 1e-20, None, ALU.max))
            dve.wait_ge(ssq_root, 1)
            chain(dve.tensor_tensor(HSC[:, :], SSQ[:, 0, :], SSQ[:, 1, :], ALU.mult))
            chain(dve.tensor_scalar(HSC[:, :], HSC[:, :], 2.0 ** 15 / (D * QUANT * QUANT) * 0.99, None, ALU.mult))
            chain(dve.tensor_scalar(HSC[:, :].bitcast(U32), HSC[:, :].bitcast(U32), 0x7F800000, None,
                                    ALU.bitwise_and))
            chain(dve.tensor_scalar(HSM[:, :], HSC[:, :], QUANT / XS, None, ALU.mult))
            dve.reciprocal(HSI[:, :], HSC[:, :]).then_inc(const_ready, 1)
            dve.wait_ge(ld["i"], 16)
            chain(dve.tensor_reduce(RMX[:, :], NI, AX.X, ALU.max, apply_absolute_value=True))
            chain(dve.tensor_scalar(RMX[:, :], RMX[:, :], 1e-25, None, ALU.max))
            chain(dve.reciprocal(RSC[:, :], RMX[:, :]))
            chain(dve.tensor_scalar(RSC[:, :], RSC[:, :], 512.0, None, ALU.mult))
            chain(dve.tensor_scalar(RSC[:, :].bitcast(U32), RSC[:, :].bitcast(U32), 0x7F800000, None,
                                    ALU.bitwise_and))
            chain(dve.reciprocal(RIV[:, :], RSC[:, :]))
            chain(dve.tensor_scalar(RIV[:, :], RIV[:, :], 1.0 / XS, None, ALU.mult))
            for c in range(2 * IC):
                ins = dve.tensor_scalar(NIS[:, c, :], NI[:, c, :], RSC[:, c:c + 1], None, ALU.mult)
            ins.then_inc(in_scaled, 1)
            dve.wait_ge(exp_a, 1)
            chain(dve.tensor_scalar(A[:, :], EP[:, 0:1], -1.0, None, ALU.mult))
            dve.tensor_copy(NA[:, :], EP[:, 0:1])
            chain(dve.tensor_scalar(NM[:, :], EP[:, 0:1], 1e-8, None, ALU.is_le))
            chain(dve.tensor_copy(IA[:, :], A[:, :]))
            dve.wait_ge(zeroed, 2)
            chain(dve.copy_predicated(IA[:, :], NM[:, :], ONE[:, :]))
            dve.reciprocal(IA[:, :], IA[:, :]).then_inc(const_ready, 1)
            for j in range(4):
                kc, half = j // 2, j % 2
                b = FILL_AT[("i", j)][0]
                dve.wait_ge(w_hi, j + 1)
                dve.tensor_tensor(WIL[:, kc, 512 * half:512 * (half + 1)], q[b][:, :],
                                  WIH[:, kc, 512 * half:512 * (half + 1)], ALU.subtract).then_inc(w_free[b], 1)
            for s in S2:
                dve.memset(XI[s][:, :, 0:TAPS - 1], 0.0).then_inc(zeroed, 1)
            dve.wait_ge(zeroed, 4)
            dve.wait_ge(const_ready, 2)
            for j in range(RING):
                dve.wait_ge(w_free[j], FILLS_OF[j])

            def body(i):
                norm_lo(i, NORM_A, 0)
                norm_lo(i, NORM_A, 1)
                hidden(i, 0, 0)
                hidden(i, 0, 1)
                residual(i, NORM_A, 0)
                norm_stats(i, NORM_B, 0)
                residual(i, NORM_A, 1)
                norm_stats(i, NORM_B, 1)
                norm_lo(i, NORM_B, 0)
                norm_lo(i, NORM_B, 1)
                conv(i, 0)
                conv(i, 1)
                delta(i, 0)
                scan(i, 0)
                delta(i, 1)
                scan(i, 1)
                skip_y(i, 0)
                residual(i, NORM_B, 0)
                norm_stats(i, NORM_C, 0)
                skip_y(i, 1)
                residual(i, NORM_B, 1)
                norm_stats(i, NORM_C, 1)
                norm_lo(i, NORM_C, 0)
                hidden(i, 1, 0)
                norm_lo(i, NORM_C, 1)

            with dve.Fori(0, STEPS - 1) as i:
                body(i)
                norm_stats(i + 1, NORM_A, 0)
                norm_stats(i + 1, NORM_A, 1)
                hidden(i, 1, 1)
                residual(i, NORM_C, 0)
                residual(i, NORM_C, 1)
            body(STEPS - 1)
            hidden(STEPS - 1, 1, 1)
            residual(STEPS - 1, NORM_C, 0)
            residual(STEPS - 1, NORM_C, 1)

        @block.tensor
        def _(pe):
            pe.wait_ge(idn_ready, 1)

            def turn(dst, src, ident=None):
                return pe.transpose(dst, src, IDN[:, :] if ident is None else ident)

            def free_bank(f):
                j, k = FILL_AT[f]
                if k:
                    pe.wait_ge(w_free[j], k)
                return j

            for name, nat, ready in (("g", NG, cast_g), ("u", NU, cast_u)):
                pe.wait_ge(ready, 1)
                for f in range(3):
                    j = free_bank((name, f))
                    for n in range(4):
                        kc, c = n // 2, 2 * f + n % 2
                        ins = turn(q[j][:, P * n:P * (n + 1)], nat[:, c, P * kc:P * (kc + 1)])
                    ins.then_inc(w_full[j], 1)
            pe.wait_ge(cast_d, 1)
            for f in range(3):
                j = free_bank(("d", f))
                for n in range(4):
                    c, a = 2 * f + n // 2, n % 2
                    ins = turn(q[j][:, P * n:P * (n + 1)], ND[:, a, P * c:P * (c + 1)])
                ins.then_inc(w_full[j], 1)
            pe.wait_ge(in_scaled, 1)
            for f in range(4):
                j = free_bank(("i", f))
                kc, half = f // 2, f % 2
                for n in range(4):
                    ins = turn(q[j][:, P * n:P * (n + 1)], NIS[:, 4 * half + n, P * kc:P * (kc + 1)])
                ins.then_inc(w_full[j], 1)
            pe.wait_ge(ld["x"], 16)
            j = free_bank(("x", 0))
            for n in range(4):
                ins = turn(q[j][:, P * n:P * (n + 1)], NX[:, P * n:P * (n + 1)])
            ins.then_inc(w_full[j], 1)
            pe.wait_ge(ld["dt"], 32)
            turn(tp[0][0:RANK, 0:N], DTN[:, :]).then_inc(dt_turned, 1)
            pe.wait_ge(dtt_ready, 1)
            j = free_bank(("dt", 0))
            for n in range(4):
                ins = pe.matmul(q[j][:, P * n:P * (n + 1)], XPD[:, P * n:P * (n + 1)], DTT[:, :],
                                start=True, stop=True)
            ins.then_inc(w_full[j], 1)
            pe.wait_ge(ld["c"], 16)
            j = free_bank(("c", 0))
            for n in range(4):
                ins = turn(q[j][:, P * n:P * (n + 1)], NC[:, n, :])
            ins.then_inc(w_full[j], 1)
            pe.wait_ge(ld["o"], 16)
            for f in range(2):
                j = free_bank(("o", f))
                for n in range(4):
                    m, a = 2 * f + n // 2, n % 2
                    ins = turn(q[j][:, P * n:P * (n + 1)], NO[:, a, P * m:P * (m + 1)])
                ins.then_inc(w_full[j], 1)
            for j in range(RING):
                pe.wait_ge(w_free[j], FILLS_OF[j])

            def turn_norm(i, k, s):
                u = 2 * k + s
                pe.wait_ge(xn_ready, 6 * i + u + 1)
                for kc in range(KD):
                    pe.wait_ge(t_lo[kc], LEAD + 6 * i + u)
                    for b in range(NB):
                        ins = turn(tp[kc][:, P * b:P * (b + 1)], XN[s][:, b, P * kc:P * (kc + 1)])
                    ins.then_inc(t_full[kc], 1)

            def open_bank(i, key):
                bank, use = Q[key]
                if use == 0:
                    pe.wait_ge(sg_ready, LEAD + 24 * i)
                    pe.wait_ge(h_ready, LEAD + 24 * i)
                    return bank
                stage, *args, n = HELD[(bank, use - 1)]
                if stage == "gu":
                    pe.wait_ge(h_ready if n % 2 else sg_ready, LEAD + 24 * i + HC * (2 * args[0] + args[1]) + n // 2 + 1)
                elif stage == "xp":
                    pe.wait_ge(pc_ready if n else bm_ready, 2 * i + args[0] + 1)
                else:
                    pe.wait_ge({"ix": xi_ready, "iz": sz_ready, "cp": yu_half}[stage],
                               2 * IC * i + IC * args[0] + n + 1)
                return bank

            def product(bank, terms):
                for n, (w, a) in enumerate(terms):
                    ins = pe.matmul(q[bank][:, :], w, a, start=(n == 0), stop=(n == len(terms) - 1))
                ins.then_inc(q_full[bank], 1)

            def split_ready(i, k, s):
                for kc in range(KD):
                    pe.wait_ge(t_hi[kc], 6 * i + 2 * k + s + 1)
                    pe.wait_ge(t_lo[kc], LEAD + 6 * i + 2 * k + s + 1)

            def gate_up(i, ffn, s):
                split_ready(i, NORM_C if ffn else NORM_A, s)
                for c in range(HC):
                    for g, w in enumerate((WG, WU)):
                        bank = open_bank(i, ("gu", ffn, s, 2 * c + g))
                        product(bank, [(w[:, kc, P * c:P * (c + 1)], part[s][:, kc, :])
                                       for part in (XH, XL) for kc in range(KD)])

            def in_proj(i, z, s):
                split_ready(i, NORM_B, s)
                for m in range(IC):
                    bank = open_bank(i, ("iz" if z else "ix", s, m))
                    col = slice(INNER * z + P * m, INNER * z + P * (m + 1))
                    product(bank, [(w[:, kc, col], part[s][:, kc, :])
                                   for w, part in ((WIH, XH), (WIL, XH), (WIH, XL)) for kc in range(KD)])

            def x_proj(i, s):
                pe.wait_ge(conv_step, TAPS * (2 * IC * i + IC * (s + 1)))
                for g, w in enumerate((WXB, WXD)):
                    bank = open_bank(i, ("xp", s, g))
                    product(bank, [(w[:, m, :], XC[s][:, m, :]) for m in range(IC)])

            def c_proj(i, s):
                pe.wait_ge(hs_ready, 2 * i + s + 1)
                for m in range(IC):
                    bank = open_bank(i, ("cp", s, m))
                    product(bank, [(WC[:, P * m:P * (m + 1)], HS[s][:, :])])

            def onto_tokens(i, k, s, terms):
                for j in range(2):
                    pe.wait_ge(res_done, LEAD + 12 * i + max(2 * (2 * k + s) + j - 1, 0))
                    for b in range(2):
                        tok = slice(P * (2 * j + b), P * (2 * j + b + 1))
                        for n, (a, c, w) in enumerate(terms):
                            ins = pe.matmul(dp[j][:, D * b:D * (b + 1)], a[:, c, tok], w[:, c, :],
                                            start=(n == 0), stop=(n == len(terms) - 1))
                    ins.then_inc(d_full[j], 1)

            def down(i, ffn, s):
                n = HC * (2 * ffn + s + 1)
                pe.wait_ge(hh_ready, 24 * i + n)
                pe.wait_ge(hl_ready, LEAD + 24 * i + n)
                onto_tokens(i, NORM_C if ffn else NORM_A, s, [(a[s], c, WD) for a in (HH, HL) for c in range(HC)])

            def out_proj(i, s):
                pe.wait_ge(yu_ready, LEAD + 2 * IC * i + IC * (s + 1))
                onto_tokens(i, NORM_B, s, [(YU[s], m, WO) for m in range(IC)])

            with pe.Fori(0, STEPS) as i:
                for stage in ORDER:
                    what, args = stage[0], stage[1:]
                    if what == "T":
                        turn_norm(i, *args)
                    elif what == "gu":
                        gate_up(i, *args)
                    elif what == "dn":
                        down(i, *args)
                    elif what == "ix":
                        in_proj(i, 0, *args)
                    elif what == "iz":
                        in_proj(i, 1, *args)
                    elif what == "xp":
                        x_proj(i, *args)
                    elif what == "cp":
                        c_proj(i, *args)
                    else:
                        out_proj(i, *args)


_INS = ['L0_attn_x', 'L0_attn_in_proj_w', 'L0_attn_conv_w', 'L0_attn_conv_b', 'L0_attn_x_proj_w',
        'L0_attn_dt_proj_w', 'L0_attn_dt_proj_b', 'L0_attn_A_log', 'L0_attn_D', 'L0_attn_C_proj_w',
        'L0_attn_out_proj_w', 'L0_ffn_w_gate', 'L0_ffn_w_up', 'L0_ffn_w_down']
_OUTS = [((B, L, D), 'float32')]


def kernel(**inputs):
    import numpy as _np
    import concourse.bacc as _bacc
    from concourse import mybir as _mybir
    from concourse.bass_utils import run_bass_kernel_spmd as _run

    nc = _bacc.Bacc("TRN2", target_bir_lowering=False, num_devices=1)
    arrays, args = {}, []
    for name in _INS:
        a = _np.ascontiguousarray(inputs[name])
        arrays[f"in_{name}_dram"] = a
        args.append(nc.dram_tensor(f"in_{name}_dram", a.shape, _mybir.dt.from_np(a.dtype), kind="ExternalInput").ap())
    for i, (shape, dtype) in enumerate(_OUTS):
        dt = _mybir.dt.from_np(_np.dtype(dtype))
        args.append(nc.dram_tensor(f"out_{i}_dram", shape, dt, kind="ExternalOutput").ap())
    macaron(nc, *args)
    r = _run(nc, [arrays], core_ids=[0])
    got = tuple(r.results[0][f"out_{i}_dram"] for i in range(len(_OUTS)))
    return got[0]
```

```python
from contextlib import ExitStack

import concourse.bass as bass
from concourse import mybir

P = 128
B, L, D = 2, 2048, 256
TILE = 512
NB = TILE // P
STEPS = L // TILE
KD = D // P
HID = 768
HC = HID // P
INNER = 512
IC = INNER // P
N = 128
RANK = 16
TAPS = 4
EPS = 1e-5
QUANT = 1.0 / 127.0
XS = 256.0
SMALL = 0.0625

F32, F16, BF16, I32 = mybir.dt.float32, mybir.dt.float16, mybir.dt.bfloat16, mybir.dt.int32
U32 = mybir.dt.uint32
ALU = mybir.AluOpType
ACT = mybir.ActivationFunctionType
AX = mybir.AxisListType

RING = 4
SSM_STEPS = 8

LAST = 2 * STEPS
LOOPS = STEPS - 1


def has(part, h):
    return {"A": -1 <= h <= LAST - 2, "B": 0 <= h <= LAST - 1, "C": 1 <= h <= LAST}[part]


def tensor_order(h):
    steps = [("ix", "B"), ("turn", "C"), ("iz", "B"), ("gu", "C"), ("xp", "B"), ("turn", "A"),
             ("down", "C"), ("gu", "A"), ("cp", "B"), ("down", "A"), ("out0", "B"), ("turn", "Bnext"),
             ("out1", "B")]
    return [(what, part) for what, part in steps if has("A" if part == "Bnext" else part, h)]


def plan():
    number, reader, count = {}, {}, dict.fromkeys(("turn", "ffn", "token", "ring"), 0)

    def take(family, part, h, n=1):
        number[family, part, h] = count[family]
        count[family] += n

    for h in range(-1, LAST + 1):
        for what, part in tensor_order(h):
            if what == "turn":
                take("turn", part, h)
            elif what in ("down", "out0"):
                take("token", part, h)
            elif what != "out1":
                take("ring", what + part, h, {"gu": 2 * HC, "xp": 2}.get(what, IC))
                at = number["ring", what + part, h]
                if what == "gu":
                    take("ffn", part, h)
                    for n in range(2 * HC):
                        reader[at + n] = ("h" if n % 2 else "sg", HC * number["ffn", part, h] + n // 2 + 1)
                elif what == "xp":
                    reader[at], reader[at + 1] = ("bm", h + 1), ("pc", h + 1)
                else:
                    for n in range(IC):
                        reader[at + n] = (what, IC * h + n + 1)
    return number, reader


NUMBER, READER = plan()
PER_LOOP = {family: NUMBER[family, part, 3] - NUMBER[family, part, 1]
            for family, part in (("turn", "C"), ("ffn", "C"), ("token", "C"), ("ring", "ixB"))}
PER_LOOP |= {"sg": HC * PER_LOOP["ffn"], "h": HC * PER_LOOP["ffn"], "bm": 2, "pc": 2,
             "ix": 2 * IC, "iz": 2 * IC, "cp": 2 * IC, "half": 2}
assert PER_LOOP["ring"] % RING == 0


class Half:

    def __init__(self, h, i=0):
        self.h, self.i = h, i
        self.b, self.f = h % 2, 1 - h % 2

    def has(self, part):
        return has(part, self.h)

    def at(self, first, family):
        return first + PER_LOOP[family] * self.i

    def number(self, family, part, more=0, back=0):
        return self.at(NUMBER[family, part, self.h - back] + more, family)

    def index(self, more=0):
        return self.at(self.h + more, "half")

    def tile(self, part):
        return (self.h + 1) // 2 - (part == "C") + self.i

    def bank(self, key, n):
        at = NUMBER["ring", key, self.h] + n
        return at % RING, at // RING + 1 + PER_LOOP["ring"] // RING * self.i

    def before(self, key, n):
        at = NUMBER["ring", key, self.h] + n - RING
        if at < 0:
            return None, 0
        who, count = READER[at]
        return who, self.at(count, who)


def wait(eng, sem, value):
    if not isinstance(value, int) or value > 0:
        eng.wait_ge(sem, value)


def macaron(nc, x, in_w, conv_w, conv_b, xp_w, dt_w, dt_b, a_log, d_skip, c_w, out_w, wg, wu, wd, out):
    with ExitStack() as ctx:
        def sb(name, shape, dt=F32):
            return ctx.enter_context(nc.sbuf_tensor(name, shape, dt))

        def psum(name):
            return ctx.enter_context(nc.psum_tensor(name, [P, 512], F32))

        def sem(name):
            return ctx.enter_context(nc.semaphore(name))

        S2 = range(B)
        X = [sb(f"x{s}", [P, NB, D]) for s in S2]
        XPRE = [sb(f"xpre{s}", [P, NB, D]) for s in S2]
        XN = [sb(f"xn{s}", [P, NB, D]) for s in S2]
        XH = [sb(f"xh{s}", [P, KD, TILE], F16) for s in S2]
        XL = [sb(f"xl{s}", [P, KD, TILE], F16) for s in S2]
        HH = [sb(f"hh{s}", [P, HC, TILE], F16) for s in S2]
        HL = [sb(f"hl{s}", [P, HC, TILE], F16) for s in S2]
        XI = [sb(f"xi{s}", [P, IC, TILE + 4]) for s in S2]
        XC = [sb(f"xc{s}", [P, IC, TILE]) for s in S2]
        SZ = [sb(f"sz{s}", [P, IC, TILE]) for s in S2]
        YU = [sb(f"yu{s}", [P, IC, TILE]) for s in S2]
        HS = [sb(f"hs{s}", [P, TILE]) for s in S2]
        CARRY = sb("carry", [P, B])
        SG = sb("sg", [P, 2, TILE])
        H = sb("h", [P, 3, TILE])
        PC = sb("pc", [P, TILE])
        EP = sb("ep", [P, TILE])
        SP = sb("sp", [P, TILE])
        DL = sb("dl", [P, TILE])
        DA = sb("da", [P, TILE])
        EX = sb("ex", [P, TILE])
        BM = sb("bm", [P, TILE])
        RE = sb("re", [P, TILE])
        SER = sb("ser", [P, TILE])
        AB = sb("ab", [P, TILE])
        BB = sb("bb", [P, TILE])
        ST, MV, MN, VO, VI, VE, RS = ({k: sb(f"{name}_{k}", [P, NB, *w]) for k in ("A", "Bnext", "C")}
                                      for name, w in (("st", [6]), ("mv", [3]), ("mn", []), ("vo", []),
                                                      ("vi", []), ("ve", []), ("rs", [])))
        NEGH = sb("negh", [P, 2 * HC])
        IDN = sb("idn", [P, P])
        WG = sb("wg", [P, KD, HID], BF16)
        WU = sb("wu", [P, KD, HID], BF16)
        WD = sb("wd", [P, HC, D], BF16)
        WIH = sb("wih", [P, KD, 2 * INNER], F16)
        WIL = sb("wil", [P, KD, 2 * INNER], F16)
        WXB = sb("wxb", [P, IC, N])
        WXD = sb("wxd", [P, IC, N])
        WC = sb("wc", [P, INNER])
        WO = sb("wo", [P, IC, D])
        CW = sb("cw", [P, IC, TAPS])
        CB = sb("cb", [P, IC])
        DS = sb("ds", [P, IC])
        DTB = sb("dtb", [P, 1])
        AL = sb("al", [P, 1])
        A = sb("a", [P, 1])
        NM = sb("nm", [P, 1], I32)
        IA = sb("ia", [P, 1])
        ONE = sb("one", [P, 1])
        NSM = sb("nsm", [P, 1])
        NA = sb("na", [P, 1])
        SSQ = sb("ssq", [P, 2, HC])
        HSC = sb("hsc", [P, HC])
        HSM = sb("hsm", [P, HC])
        HSI = sb("hsi", [P, HC])
        RMX = sb("rmx", [P, 2 * IC])
        RSC = sb("rsc", [P, 2 * IC])
        RIV = sb("riv", [P, 2 * IC])
        DTN = sb("dtn", [P, RANK])
        XPD = sb("xpd", [RANK, INNER])
        DTT = sb("dtt", [RANK, N])
        NGI = HH[0][:, :, :].bitcast(I32).rearrange("p c (u f) -> p (c u) f", f=D)
        NUI = HL[0][:, :, :].bitcast(I32).rearrange("p c (u f) -> p (c u) f", f=D)
        NDI = HH[1][:, :, :].bitcast(I32).rearrange("p c t -> p (c t)").rearrange("p (a h) -> p a h", h=HID)
        NG = SZ[0][:, 0:3, :].rearrange("p c (u f) -> p (c u) f", f=D)
        NU = SZ[1][:, 0:3, :].rearrange("p c (u f) -> p (c u) f", f=D)
        ND = YU[0][:, 0:3, :].rearrange("p c t -> p (c t)").rearrange("p (a h) -> p a h", h=HID)
        SQG = XI[0][:, 0:3, 0:512].rearrange("p c (u f) -> p c u f", f=D)
        SQU = XI[1][:, 0:3, 0:512].rearrange("p c (u f) -> p c u f", f=D)
        NI = XC[0][:, :, :].rearrange("p c (u f) -> p (c u) f", f=D)
        NIS = XC[1][:, :, :].rearrange("p c (u f) -> p (c u) f", f=D)
        NX = YU[1][:, 0, :]
        NC = YU[1][:, 1, :].rearrange("p (m n) -> p m n", n=N)
        NO = YU[1][:, 2:4, :]

        q = [psum(f"q{j}") for j in range(RING)]
        tp = [psum(f"tp{j}") for j in range(KD)]
        dp = [psum(f"dp{j}") for j in range(2)]

        ld_x = [sem(f"ld_x{s}") for s in S2]
        ld = {n: sem("ld_" + n) for n in ("g", "u", "d", "i", "x", "c", "o", "dt", "small")}
        st_y = [sem(f"st_y{s}") for s in S2]
        idn_zero, idn_ready = sem("idn_zero"), sem("idn_ready")
        cast_g, cast_u, cast_d = sem("cast_g"), sem("cast_u"), sem("cast_d")
        sq_u = sem("sq_u")
        in_scaled = sem("in_scaled")
        w_full = [sem(f"w_full{j}") for j in range(RING)]
        w_hi = sem("w_hi")
        w_free = [sem(f"w_free{j}") for j in range(RING)]
        dt_turned = sem("dt_turned")
        dtt_ready = sem("dtt_ready")
        small = sem("small")
        exp_a = sem("exp_a")
        const_ready = sem("const_ready")
        zeroed = sem("zeroed")
        res_done = sem("res_done")
        ln_step, rs_ready = sem("ln_step"), sem("rs_ready")
        negh_ready, ssq_root = sem("negh_ready"), sem("ssq_root")
        xn_ready = sem("xn_ready")
        t_full = [sem(f"t_full{j}") for j in range(KD)]
        t_hi = [sem(f"t_hi{j}") for j in range(KD)]
        t_lo = [sem(f"t_lo{j}") for j in range(KD)]
        q_full = [sem(f"q_full{j}") for j in range(RING)]
        d_full = [sem(f"d_full{j}") for j in range(2)]
        sg_ready, h_ready, hh_ready, hl_ready = sem("sg_ready"), sem("h_ready"), sem("hh_ready"), sem("hl_ready")
        xi_ready, xi_free, conv_step = sem("xi_ready"), sem("xi_free"), sem("conv_step")
        sz_ready, yu_half, yu_ready = sem("sz_ready"), sem("yu_half"), sem("yu_ready")
        pc_ready, ep_ready, sp_ready = sem("pc_ready"), sem("ep_ready"), sem("sp_ready")
        ex_ready, bm_ready = sem("ex_ready"), sem("bm_ready")
        ssm_step, hs_ready, carried = sem("ssm_step"), sem("hs_ready"), sem("carried")

        def xrows(s, t):
            return x[s, bass.ds(t * TILE, TILE), :].rearrange("(b p) d -> p b d", p=P)

        def orows(s, t):
            return out[s, bass.ds(t * TILE, TILE), :].rearrange("(b p) d -> p b d", p=P)

        FILLS = ([("g", j) for j in range(3)] + [("u", j) for j in range(3)] + [("d", j) for j in range(3)]
                 + [("i", j) for j in range(4)] + [("x", 0), ("dt", 0), ("c", 0), ("o", 0), ("o", 1)])
        FILL_AT = {f: (n % RING, n // RING) for n, f in enumerate(FILLS)}
        FILLS_OF = [sum(1 for n in range(len(FILLS)) if n % RING == j) for j in range(RING)]

        block = ctx.enter_context(nc.Block())

        @block.sync
        def _(sp):
            for s in S2:
                sp.dma_start(XPRE[s][:, :, :], xrows(s, 0)).then_inc(ld_x[s], 16)
            sp.dma_start(NUI, wu.rearrange("(c p) f -> p c f", p=P)).then_inc(ld["u"], 16)
            sp.dma_start(NI, in_w.rearrange("(c p) f -> p c f", p=P)).then_inc(ld["i"], 16)
            sp.dma_start(NX, xp_w[RANK:RANK + N, :]).then_inc(ld["x"], 16)
            sp.dma_start(XPD[:, :], xp_w[0:RANK, :]).then_inc(ld["dt"], 16)
            sp.dma_start(NC, c_w.rearrange("(m p) n -> p m n", p=P)).then_inc(ld["c"], 16)
            sp.dma_start(NO, out_w.rearrange("(a p) i -> p a i", p=P)).then_inc(ld["o"], 16)

            def half(g):
                if g.has("A") and g.h > 0:
                    sp.wait_ge(res_done, 2 * g.number("token", "A", back=2) + 2)
                    sp.dma_start(XPRE[g.f][:, :, :], xrows(g.f, g.tile("A"))).then_inc(ld_x[g.f], 16)
                if g.has("C"):
                    sp.wait_ge(res_done, 2 * g.number("token", "C") + 2)
                    sp.dma_start(orows(g.f, g.tile("C")), X[g.f][:, :, :]).then_inc(st_y[g.f], 16)

            with sp.Fori(0, LOOPS) as i:
                half(Half(1, i))
                half(Half(2, i))
            half(Half(LAST - 1))
            half(Half(LAST))
            for s in S2:
                sp.wait_ge(st_y[s], 16 * STEPS)

        @block.gpsimd
        def _(pool):
            pool.memset(IDN[:, :], 0.0).then_inc(idn_zero, 1)
            pool.wait_ge(idn_zero, 1)
            pool.affine_select(out=IDN[:, :], in_=IDN[:, :], compare_op=ALU.not_equal, fill=1.0, base=0,
                               pattern=[[-1, P]], channel_multiplier=1).then_inc(idn_ready, 1)
            pool.memset(NEGH[:, :], -0.5).then_inc(negh_ready, 1)

            def root(g, k):
                pool.wait_ge(ln_step, 4 * g.number("turn", k) + 4)
                pool.tensor_tensor(RS[k][:, :], VE[k][:, :], NEGH[:, 0:NB], ALU.pow).then_inc(rs_ready, 1)

            pool.wait_ge(negh_ready, 1)
            pool.wait_ge(cast_u, 1)
            pool.tensor_tensor(SQU, NU.rearrange("p (a u) f -> p a u f", u=2),
                               NU.rearrange("p (a u) f -> p a u f", u=2), ALU.mult).then_inc(sq_u, 1)
            pool.wait_ge(ld["d"], 16)
            pool.tensor_copy(ND, NDI).then_inc(cast_d, 1)
            root(Half(-1), "A")
            pool.wait_ge(small, 4)
            pool.tensor_tensor(SSQ[:, :, :].rearrange("p a c -> p (a c)"),
                               SSQ[:, :, :].rearrange("p a c -> p (a c)"), NEGH[:, :], ALU.pow)\
                .then_inc(ssq_root, 1)

            def hidden_low(g, k):
                for c in range(HC):
                    pool.wait_ge(hh_ready, HC * g.number("ffn", k) + c + 1)
                    j = (HC * NUMBER["ffn", k, g.h] + c) % 3
                    pool.tensor_tensor(HL[g.f][:, c, :], H[:, j, :], HH[g.f][:, c, :], ALU.subtract)\
                        .then_inc(hl_ready, 1)

            def gate_y(g):
                for m in range(IC):
                    pool.wait_ge(sz_ready, IC * g.index() + m + 1)
                    pool.wait_ge(yu_half, IC * g.index() + m + 1)
                    pool.tensor_tensor(YU[g.b][:, m, :], YU[g.b][:, m, :], SZ[g.b][:, m, :], ALU.mult)\
                        .then_inc(yu_ready, 1)

            def half(g):
                if g.has("C"):
                    root(g, "C")
                    hidden_low(g, "C")
                if g.has("A"):
                    if g.h >= 0:
                        root(g, "A")
                    hidden_low(g, "A")
                if g.has("B"):
                    gate_y(g)
                if g.has("A"):
                    root(g, "Bnext")

            half(Half(-1))
            half(Half(0))
            with pool.Fori(0, LOOPS) as i:
                half(Half(1, i))
                half(Half(2, i))
            half(Half(LAST - 1))
            half(Half(LAST))

        @block.scalar
        def _(act):
            act.dma_start(NGI, wg.rearrange("(c p) f -> p c f", p=P)).then_inc(ld["g"], 16)
            act.dma_start(NDI, wd.rearrange("(a p) h -> p a h", p=P)).then_inc(ld["d"], 16)
            act.dma_start(DTN[:, :], dt_w).then_inc(ld["dt"], 16)
            act.dma_start(CW[:, :, :], conv_w.rearrange("(m p) o k -> p m (o k)", p=P)).then_inc(ld["small"], 16)
            act.dma_start(CB[:, :], conv_b.rearrange("(m p) -> p m", p=P), allow_slow_non_contiguous=True).then_inc(ld["small"], 16)
            act.dma_start(DS[:, :], d_skip.rearrange("(m p) -> p m", p=P), allow_slow_non_contiguous=True).then_inc(ld["small"], 16)
            act.dma_start(DTB[:, :], dt_b.rearrange("(p o) -> p o", o=1)).then_inc(ld["small"], 16)
            act.dma_start(AL[:, :], a_log.rearrange("(p o) -> p o", o=1)).then_inc(ld["small"], 16)
            act.wait_ge(ld["g"], 16)
            act.activation(NG, NGI, ACT.Copy).then_inc(cast_g, 1)
            act.wait_ge(ld["small"], 80)
            act.activation(EP[:, 0:1], AL[:, :], ACT.Exp).then_inc(exp_a, 1)

            def fill(f, dst, src, scale=None):
                j, k = FILL_AT[f]
                act.wait_ge(w_full[j], k + 1)
                return act.activation(dst, src, ACT.Copy, **({} if scale is None else {"scale": scale}))

            for j in range(3):
                fill(("g", j), WG[:, :, 2 * P * j:2 * P * (j + 1)],
                     q[FILL_AT[("g", j)][0]][:, :].rearrange("p (k h) -> p k h", k=KD))\
                    .then_inc(w_free[FILL_AT[("g", j)][0]], 1)
            for j in range(3):
                fill(("u", j), WU[:, :, 2 * P * j:2 * P * (j + 1)],
                     q[FILL_AT[("u", j)][0]][:, :].rearrange("p (k h) -> p k h", k=KD))\
                    .then_inc(w_free[FILL_AT[("u", j)][0]], 1)
            act.wait_ge(const_ready, 1)
            for j in range(3):
                b = FILL_AT[("d", j)][0]
                fill(("d", j), WD[:, 2 * j, :], q[b][:, 0:D], HSI[:, 2 * j:2 * j + 1])
                act.activation(WD[:, 2 * j + 1, :], q[b][:, D:2 * D], ACT.Copy,
                               scale=HSI[:, 2 * j + 1:2 * j + 2]).then_inc(w_free[b], 1)
            for j in range(4):
                kc, half = j // 2, j % 2
                b = FILL_AT[("i", j)][0]
                fill(("i", j), WIH[:, kc, 512 * half:512 * (half + 1)], q[b][:, :]).then_inc(w_hi, 1)
            fill(("x", 0), WXB[:, :, :].rearrange("p k n -> p (k n)"), q[FILL_AT[("x", 0)][0]][:, :])\
                .then_inc(w_free[FILL_AT[("x", 0)][0]], 1)
            act.wait_ge(dt_turned, 1)
            act.activation(DTT[:, :], tp[0][0:RANK, 0:N], ACT.Copy).then_inc(dtt_ready, 1)
            fill(("dt", 0), WXD[:, :, :].rearrange("p k n -> p (k n)"), q[FILL_AT[("dt", 0)][0]][:, :])\
                .then_inc(w_free[FILL_AT[("dt", 0)][0]], 1)
            fill(("c", 0), WC[:, :], q[FILL_AT[("c", 0)][0]][:, :]).then_inc(w_free[FILL_AT[("c", 0)][0]], 1)
            for j in range(2):
                b = FILL_AT[("o", j)][0]
                fill(("o", j), WO[:, 2 * j:2 * j + 2, :], q[b][:, :].rearrange("p (k h) -> p k h", k=2))\
                    .then_inc(w_free[b], 1)
            act.wait_ge(const_ready, 2)
            act.wait_ge(zeroed, 2)

            def norm_hi(g, k):
                for kc in range(KD):
                    act.wait_ge(t_full[kc], g.number("turn", k) + 1)
                    act.activation(XH[g.f][:, kc, :], tp[kc][:, :], ACT.Copy, scale=XS).then_inc(t_hi[kc], 1)

            def hidden(g, k):
                first = HC * NUMBER["ffn", k, g.h]
                for c in range(HC + 1):
                    n = HC * g.number("ffn", k) + c
                    if c < HC:
                        bank, uses = g.bank("gu" + k, 2 * c)
                        act.wait_ge(q_full[bank], uses)
                        wait(act, h_ready, n - 1)
                        act.activation(SG[:, (first + c) % 2, :], q[bank][:, :], ACT.Silu, scale=QUANT / XS)\
                            .then_inc(sg_ready, 1)
                    if c > 0:
                        act.wait_ge(h_ready, n)
                        act.activation(HH[g.f][:, c - 1, :], H[:, (first + c - 1) % 3, :], ACT.Copy)\
                            .then_inc(hh_ready, 1)

            def conv_in(g):
                wait(act, xi_free, g.index(-1))
                for m in range(IC):
                    bank, uses = g.bank("ixB", m)
                    act.wait_ge(q_full[bank], uses)
                    act.activation(XI[g.b][:, m, TAPS - 1:TAPS - 1 + TILE], q[bank][:, :], ACT.Copy,
                                   scale=RIV[:, m:m + 1]).then_inc(xi_ready, 1)

            def silu_z(g):
                wait(act, yu_ready, IC * g.index(-1))
                for m in range(IC):
                    bank, uses = g.bank("izB", m)
                    act.wait_ge(q_full[bank], uses)
                    act.activation(SZ[g.b][:, m, :], q[bank][:, :], ACT.Silu,
                                   scale=RIV[:, IC + m:IC + m + 1]).then_inc(sz_ready, 1)

            def softplus(g):
                bank, uses = g.bank("xpB", 0)
                act.wait_ge(q_full[bank], uses)
                act.activation(BM[:, :], q[bank][:, :], ACT.Copy, scale=IA[:, 0:1]).then_inc(bm_ready, 1)
                act.wait_ge(pc_ready, g.index(1))
                act.activation(EP[:, :], PC[:, :], ACT.Exp).then_inc(ep_ready, 1)
                act.wait_ge(ep_ready, g.index(1))
                act.activation(SP[:, :], EP[:, :], ACT.Ln, bias=ONE[:, 0:1]).then_inc(sp_ready, 1)

            def decay(g):
                act.wait_ge(ssm_step, SSM_STEPS * g.index() + 1)
                act.activation(RE[:, :], DL[:, :], ACT.Relu, bias=NSM[:, 0:1], scale=NA[:, 0:1])\
                    .then_inc(ex_ready, 1)
                act.wait_ge(ex_ready, 2 * g.index() + 1)
                act.activation(EX[:, :], RE[:, :], ACT.Exp, scale=-1.0).then_inc(ex_ready, 1)

            def half(g):
                if g.has("B"):
                    conv_in(g)
                if g.has("C"):
                    norm_hi(g, "C")
                if g.has("B"):
                    silu_z(g)
                if g.has("C"):
                    hidden(g, "C")
                if g.has("B"):
                    softplus(g)
                if g.has("A"):
                    norm_hi(g, "A")
                if g.has("B"):
                    decay(g)
                if g.has("A"):
                    hidden(g, "A")
                    norm_hi(g, "Bnext")

            half(Half(-1))
            half(Half(0))
            with act.Fori(0, LOOPS) as i:
                half(Half(1, i))
                half(Half(2, i))
            half(Half(LAST - 1))
            half(Half(LAST))

        @block.vector
        def _(dve):
            dve.memset(CARRY[:, :], 0.0).then_inc(zeroed, 1)
            dve.memset(NSM[:, :], -SMALL)
            dve.memset(ONE[:, :], 1.0).then_inc(zeroed, 1)

            def stats(g, k, blocks):
                if k == "A":
                    dve.wait_ge(ld_x[g.f], 16 * g.tile("A") + 16)
                else:
                    before = g.number("token", "A") if k == "Bnext" else g.number("token", "B", back=1)
                    dve.wait_ge(res_done, 2 * before + 1 + (blocks[0] > 0))
                src = XPRE[g.f] if k == "A" else X[g.f]
                for b in blocks:
                    ins = dve.bn_stats(ST[k][:, b, :], src[:, b, :])
                if blocks[-1] == NB - 1:
                    ins.then_inc(ln_step, 1)

            def variance(g, k):
                at = 4 * g.number("turn", k)
                dve.wait_ge(ln_step, at + 1)
                dve.tensor_tensor(MV[k][:, :, 0], ST[k][:, :, 1], ST[k][:, :, 4], ALU.add)
                dve.tensor_tensor(MV[k][:, :, 1], ST[k][:, :, 1], ST[k][:, :, 4], ALU.subtract)
                dve.tensor_tensor(MV[k][:, :, 2], ST[k][:, :, 2], ST[k][:, :, 5], ALU.add).then_inc(ln_step, 1)
                dve.wait_ge(ln_step, at + 2)
                dve.tensor_scalar(MN[k][:, :], MV[k][:, :, 0], 0.5, None, ALU.mult)
                dve.scalar_tensor_tensor(out=VO[k][:, :], in0=MV[k][:, :, 1], scalar=0.25, in1=MV[k][:, :, 1],
                                         op0=ALU.mult, op1=ALU.mult)
                dve.tensor_scalar(VI[k][:, :], MV[k][:, :, 2], 1.0 / D, EPS, ALU.mult, ALU.add)\
                    .then_inc(ln_step, 1)
                dve.wait_ge(ln_step, at + 3)
                dve.tensor_tensor(VE[k][:, :], VO[k][:, :], VI[k][:, :], ALU.add).then_inc(ln_step, 1)

            def normalize(g, k):
                src = XPRE[g.f] if k == "A" else X[g.f]
                dve.wait_ge(rs_ready, g.number("turn", k, 1))
                for b in range(NB):
                    ins = dve.tensor_scalar(XN[g.f][:, b, :], src[:, b, :], MN[k][:, b:b + 1],
                                            RS[k][:, b:b + 1], ALU.subtract, ALU.mult)
                ins.then_inc(xn_ready, 1)

            def norm_lo(g, k):
                for kc in range(KD):
                    dve.wait_ge(t_hi[kc], g.number("turn", k, 1))
                    dve.scalar_tensor_tensor(out=XL[g.f][:, kc, :], in0=tp[kc][:, :], scalar=XS,
                                             in1=XH[g.f][:, kc, :], op0=ALU.mult, op1=ALU.subtract)\
                        .then_inc(t_lo[kc], 1)

            def hidden(g, k, chunks):
                for c in chunks:
                    n = HC * g.number("ffn", k) + c
                    first = HC * NUMBER["ffn", k, g.h] + c
                    bank, uses = g.bank("gu" + k, 2 * c + 1)
                    dve.wait_ge(q_full[bank], uses)
                    dve.wait_ge(sg_ready, n + 1)
                    wait(dve, hl_ready, n - 2)
                    dve.scalar_tensor_tensor(out=H[:, first % 3, :], in0=SG[:, first % 2, :],
                                             scalar=HSM[:, c:c + 1], in1=q[bank][:, :],
                                             op0=ALU.mult, op1=ALU.mult).then_inc(h_ready, 1)

            def residual(g, k, j, back=0):
                s = g.b if k == "B" else g.f
                if back:
                    s = g.f
                if k == "A":
                    wait(dve, st_y[s], 16 * g.tile("A"))
                dve.wait_ge(d_full[j], g.number("token", k, 1, back))
                src = XPRE[s] if k == "A" else X[s]
                dve.scalar_tensor_tensor(
                    out=X[s][:, 2 * j:2 * j + 2, :], in0=dp[j][:, :].rearrange("p (b d) -> p b d", d=D),
                    scalar=1.0 if k == "B" else 0.5 * QUANT, in1=src[:, 2 * j:2 * j + 2, :],
                    op0=ALU.mult, op1=ALU.add).then_inc(res_done, 1)

            def conv(g, m, taps):
                s = g.b
                for k in taps:
                    if k == TAPS - 1:
                        dve.wait_ge(xi_ready, IC * g.index() + m + 1)
                        dve.tensor_scalar(XC[s][:, m, :], XI[s][:, m, k:k + TILE], CW[:, m, k:k + 1],
                                          CB[:, m:m + 1], ALU.mult, ALU.add).then_inc(conv_step, 1)
                    else:
                        dve.wait_ge(conv_step, TAPS * (IC * g.index() + m) + TAPS - 1 - k)
                        dve.scalar_tensor_tensor(out=XC[s][:, m, :], in0=XI[s][:, m, k:k + TILE],
                                                 scalar=CW[:, m, k:k + 1], in1=XC[s][:, m, :],
                                                 op0=ALU.mult, op1=ALU.add).then_inc(conv_step, 1)
                if m == IC - 1 and taps[-1] == 0:
                    dve.wait_ge(conv_step, TAPS * IC * g.index(1))
                    dve.tensor_copy(XI[s][:, :, 0:TAPS - 1], XI[s][:, :, TILE:TILE + TAPS - 1])\
                        .then_inc(xi_free, 1)

            def delta_in(g):
                bank, uses = g.bank("xpB", 1)
                dve.wait_ge(q_full[bank], uses)
                dve.tensor_scalar(PC[:, :], q[bank][:, :], DTB[:, 0:1], 0.0, ALU.add, ALU.min)\
                    .then_inc(pc_ready, 1)

            def delta(g):
                dve.wait_ge(sp_ready, g.index(1))
                dve.tensor_scalar(DL[:, :], SP[:, :], 0.001, 0.1, ALU.max, ALU.min).then_inc(ssm_step, 1)
                dve.wait_ge(ssm_step, SSM_STEPS * g.index() + 1)
                dve.tensor_scalar(DA[:, :], DL[:, :], A[:, 0:1], -SMALL, ALU.mult, ALU.max).then_inc(ssm_step, 1)

            def series(g):
                at = SSM_STEPS * g.index()
                dve.wait_ge(ssm_step, at + 2)
                dve.scalar_tensor_tensor(out=SER[:, :], in0=DA[:, :], scalar=4.0, in1=DA[:, :],
                                         op0=ALU.add, op1=ALU.mult).then_inc(ssm_step, 1)
                dve.wait_ge(ssm_step, at + 3)
                dve.scalar_tensor_tensor(out=SER[:, :], in0=SER[:, :], scalar=12.0, in1=DA[:, :],
                                         op0=ALU.add, op1=ALU.mult).then_inc(ssm_step, 1)
                dve.wait_ge(ssm_step, at + 4)
                dve.scalar_tensor_tensor(out=SER[:, :], in0=SER[:, :], scalar=24.0, in1=DA[:, :],
                                         op0=ALU.add, op1=ALU.mult).then_inc(ssm_step, 1)
                dve.wait_ge(ssm_step, at + 5)
                dve.tensor_scalar(SER[:, :], SER[:, :], 1.0 / 24.0, 1.0, ALU.mult, ALU.add).then_inc(ssm_step, 1)

            def coefficients(g):
                at = SSM_STEPS * g.index()
                dve.wait_ge(ssm_step, at + 6)
                dve.wait_ge(ex_ready, 2 * g.index(1))
                dve.tensor_tensor(AB[:, :], SER[:, :], EX[:, :], ALU.mult).then_inc(ssm_step, 1)
                dve.wait_ge(ssm_step, at + 7)
                dve.wait_ge(bm_ready, g.index(1))
                dve.scalar_tensor_tensor(out=BB[:, :], in0=AB[:, :], scalar=-1.0, in1=BM[:, :],
                                         op0=ALU.add, op1=ALU.mult).then_inc(ssm_step, 1)

            def scan(g):
                s = g.b
                dve.wait_ge(ssm_step, SSM_STEPS * g.index(1))
                wait(dve, carried, g.index())
                dve.tensor_tensor_scan(HS[s][:, :], AB[:, :], BB[:, :], CARRY[:, s:s + 1],
                                       ALU.mult, ALU.add).then_inc(hs_ready, 1)
                dve.wait_ge(hs_ready, g.index(1))
                dve.tensor_copy(CARRY[:, s:s + 1], HS[s][:, TILE - 1:TILE]).then_inc(carried, 1)

            def skip_y(g):
                for m in range(IC):
                    bank, uses = g.bank("cpB", m)
                    dve.wait_ge(q_full[bank], uses)
                    dve.scalar_tensor_tensor(out=YU[g.b][:, m, :], in0=XC[g.b][:, m, :], scalar=DS[:, m:m + 1],
                                             in1=q[bank][:, :], op0=ALU.mult, op1=ALU.add)\
                        .then_inc(yu_half, 1)

            dve.wait_ge(ld["u"], 16)
            dve.tensor_copy(NU, NUI).then_inc(cast_u, 1)
            stats(Half(-1), "A", range(NB))
            variance(Half(-1), "A")
            normalize(Half(-1), "A")
            step = [0]

            def chain(ins):
                step[0] += 1
                ins.then_inc(small, 1)
                dve.wait_ge(small, step[0])

            dve.wait_ge(cast_g, 1)
            chain(dve.tensor_tensor(SQG, NG.rearrange("p (a u) f -> p a u f", u=2),
                                    NG.rearrange("p (a u) f -> p a u f", u=2), ALU.mult))
            chain(dve.tensor_reduce(SSQ[:, 0, :].rearrange("p (a u) -> p a u", u=2), SQG, AX.X, ALU.add))
            dve.wait_ge(sq_u, 1)
            chain(dve.tensor_reduce(SSQ[:, 1, :].rearrange("p (a u) -> p a u", u=2), SQU, AX.X, ALU.add))
            chain(dve.tensor_scalar(SSQ[:, :, :], SSQ[:, :, :], 1e-20, None, ALU.max))
            dve.wait_ge(ssq_root, 1)
            chain(dve.tensor_tensor(HSC[:, :], SSQ[:, 0, :], SSQ[:, 1, :], ALU.mult))
            chain(dve.tensor_scalar(HSC[:, :], HSC[:, :], 2.0 ** 15 / (D * QUANT * QUANT) * 0.99, None, ALU.mult))
            chain(dve.tensor_scalar(HSC[:, :].bitcast(U32), HSC[:, :].bitcast(U32), 0x7F800000, None,
                                    ALU.bitwise_and))
            chain(dve.tensor_scalar(HSM[:, :], HSC[:, :], QUANT / XS, None, ALU.mult))
            dve.reciprocal(HSI[:, :], HSC[:, :]).then_inc(const_ready, 1)
            dve.wait_ge(ld["i"], 16)
            chain(dve.tensor_reduce(RMX[:, :], NI, AX.X, ALU.max, apply_absolute_value=True))
            chain(dve.tensor_scalar(RMX[:, :], RMX[:, :], 1e-25, None, ALU.max))
            chain(dve.reciprocal(RSC[:, :], RMX[:, :]))
            chain(dve.tensor_scalar(RSC[:, :], RSC[:, :], 512.0, None, ALU.mult))
            chain(dve.tensor_scalar(RSC[:, :].bitcast(U32), RSC[:, :].bitcast(U32), 0x7F800000, None,
                                    ALU.bitwise_and))
            chain(dve.reciprocal(RIV[:, :], RSC[:, :]))
            chain(dve.tensor_scalar(RIV[:, :], RIV[:, :], 1.0 / XS, None, ALU.mult))
            for c in range(2 * IC):
                ins = dve.tensor_scalar(NIS[:, c, :], NI[:, c, :], RSC[:, c:c + 1], None, ALU.mult)
            ins.then_inc(in_scaled, 1)
            dve.wait_ge(exp_a, 1)
            chain(dve.tensor_scalar(A[:, :], EP[:, 0:1], -1.0, None, ALU.mult))
            dve.tensor_copy(NA[:, :], EP[:, 0:1])
            chain(dve.tensor_scalar(NM[:, :], EP[:, 0:1], 1e-8, None, ALU.is_le))
            chain(dve.tensor_copy(IA[:, :], A[:, :]))
            dve.wait_ge(zeroed, 2)
            chain(dve.copy_predicated(IA[:, :], NM[:, :], ONE[:, :]))
            dve.reciprocal(IA[:, :], IA[:, :]).then_inc(const_ready, 1)
            for j in range(4):
                kc, half = j // 2, j % 2
                b = FILL_AT[("i", j)][0]
                dve.wait_ge(w_hi, j + 1)
                dve.tensor_tensor(WIL[:, kc, 512 * half:512 * (half + 1)], q[b][:, :],
                                  WIH[:, kc, 512 * half:512 * (half + 1)], ALU.subtract).then_inc(w_free[b], 1)
            for s in S2:
                dve.memset(XI[s][:, :, 0:TAPS - 1], 0.0).then_inc(zeroed, 1)
            dve.wait_ge(zeroed, 4)
            dve.wait_ge(const_ready, 2)
            for j in range(RING):
                dve.wait_ge(w_free[j], FILLS_OF[j])

            def half(g):
                front, rear = (0, 1), (2, 3)
                B, C, A, late = g.has("B"), g.has("C"), g.has("A"), g.h > 0
                if C:
                    residual(g, "B", 1, back=1)
                    stats(g, "C", rear)
                    variance(g, "C")
                    normalize(g, "C")
                if B:
                    conv(g, 0, (3, 2, 1, 0))
                if C:
                    norm_lo(g, "C")
                if B:
                    conv(g, 1, (3, 2, 1, 0))
                    conv(g, 2, (3, 2))
                if C:
                    hidden(g, "C", (0,))
                if B:
                    conv(g, 2, (1, 0))
                if C:
                    hidden(g, "C", (1,))
                if B:
                    conv(g, 3, (3, 2))
                if C:
                    hidden(g, "C", (2,))
                if B:
                    conv(g, 3, (1, 0))
                if C:
                    hidden(g, "C", (3,))
                if A and g.h >= 0:
                    stats(g, "A", front)
                if C:
                    hidden(g, "C", (4,))
                if A and g.h >= 0:
                    stats(g, "A", rear)
                    variance(g, "A")
                if C:
                    hidden(g, "C", (5,))
                if A and g.h >= 0:
                    normalize(g, "A")
                if B:
                    delta_in(g)
                if A:
                    norm_lo(g, "A")
                if B:
                    delta(g)
                if C:
                    residual(g, "C", 0)
                if B:
                    series(g)
                if C:
                    residual(g, "C", 1)
                if B:
                    coefficients(g)
                if A:
                    hidden(g, "A", (0,))
                if B:
                    scan(g)
                if A:
                    hidden(g, "A", (1, 2, 3, 4, 5))
                if B:
                    skip_y(g)
                if A:
                    for j in range(2):
                        residual(g, "A", j)
                        stats(g, "Bnext", (front, rear)[j])
                    variance(g, "Bnext")
                    normalize(g, "Bnext")
                if B:
                    residual(g, "B", 0)
                    if has("C", g.h + 1):
                        stats_ahead(g, front)
                if A:
                    norm_lo(g, "Bnext")

            def stats_ahead(g, blocks):
                dve.wait_ge(res_done, 2 * g.number("token", "B") + 1)
                for b in blocks:
                    dve.bn_stats(ST["C"][:, b, :], X[g.b][:, b, :])

            half(Half(-1))
            half(Half(0))
            with dve.Fori(0, LOOPS) as i:
                half(Half(1, i))
                half(Half(2, i))
            half(Half(LAST - 1))
            half(Half(LAST))

        @block.tensor
        def _(pe):
            pe.wait_ge(idn_ready, 1)

            def turn(dst, src, ident=None):
                return pe.transpose(dst, src, IDN[:, :] if ident is None else ident)

            def free_bank(f):
                j, k = FILL_AT[f]
                if k:
                    pe.wait_ge(w_free[j], k)
                return j

            for name, nat, ready in (("g", NG, cast_g), ("u", NU, cast_u)):
                pe.wait_ge(ready, 1)
                for f in range(3):
                    j = free_bank((name, f))
                    for n in range(4):
                        kc, c = n // 2, 2 * f + n % 2
                        ins = turn(q[j][:, P * n:P * (n + 1)], nat[:, c, P * kc:P * (kc + 1)])
                    ins.then_inc(w_full[j], 1)
            pe.wait_ge(cast_d, 1)
            for f in range(3):
                j = free_bank(("d", f))
                for n in range(4):
                    c, a = 2 * f + n // 2, n % 2
                    ins = turn(q[j][:, P * n:P * (n + 1)], ND[:, a, P * c:P * (c + 1)])
                ins.then_inc(w_full[j], 1)
            pe.wait_ge(in_scaled, 1)
            for f in range(4):
                j = free_bank(("i", f))
                kc, half = f // 2, f % 2
                for n in range(4):
                    ins = turn(q[j][:, P * n:P * (n + 1)], NIS[:, 4 * half + n, P * kc:P * (kc + 1)])
                ins.then_inc(w_full[j], 1)
            pe.wait_ge(ld["x"], 16)
            j = free_bank(("x", 0))
            for n in range(4):
                ins = turn(q[j][:, P * n:P * (n + 1)], NX[:, P * n:P * (n + 1)])
            ins.then_inc(w_full[j], 1)
            pe.wait_ge(ld["dt"], 32)
            turn(tp[0][0:RANK, 0:N], DTN[:, :]).then_inc(dt_turned, 1)
            pe.wait_ge(dtt_ready, 1)
            j = free_bank(("dt", 0))
            for n in range(4):
                ins = pe.matmul(q[j][:, P * n:P * (n + 1)], XPD[:, P * n:P * (n + 1)], DTT[:, :],
                                start=True, stop=True)
            ins.then_inc(w_full[j], 1)
            pe.wait_ge(ld["c"], 16)
            j = free_bank(("c", 0))
            for n in range(4):
                ins = turn(q[j][:, P * n:P * (n + 1)], NC[:, n, :])
            ins.then_inc(w_full[j], 1)
            pe.wait_ge(ld["o"], 16)
            for f in range(2):
                j = free_bank(("o", f))
                for n in range(4):
                    m, a = 2 * f + n // 2, n % 2
                    ins = turn(q[j][:, P * n:P * (n + 1)], NO[:, a, P * m:P * (m + 1)])
                ins.then_inc(w_full[j], 1)
            for j in range(RING):
                pe.wait_ge(w_free[j], FILLS_OF[j])

            def turn_norm(g, k):
                pe.wait_ge(xn_ready, g.number("turn", k, 1))
                for kc in range(KD):
                    wait(pe, t_lo[kc], g.number("turn", k))
                    for b in range(NB):
                        ins = turn(tp[kc][:, P * b:P * (b + 1)], XN[g.f][:, b, P * kc:P * (kc + 1)])
                    ins.then_inc(t_full[kc], 1)

            def split_ready(g, k, back=0):
                for kc in range(KD):
                    pe.wait_ge(t_hi[kc], g.number("turn", k, 1, back))
                    pe.wait_ge(t_lo[kc], g.number("turn", k, 1, back))

            readers = {"sg": sg_ready, "h": h_ready, "bm": bm_ready, "pc": pc_ready,
                       "ix": xi_ready, "iz": sz_ready, "cp": yu_half}

            def product(g, key, n, terms):
                who, count = g.before(key, n)
                if who:
                    pe.wait_ge(readers[who], count)
                bank = g.bank(key, n)[0]
                for at, (w, a) in enumerate(terms):
                    ins = pe.matmul(q[bank][:, :], w, a, start=(at == 0), stop=(at == len(terms) - 1))
                ins.then_inc(q_full[bank], 1)

            def gate_up(g, k):
                split_ready(g, k)
                for c in range(HC):
                    for up, w in enumerate((WG, WU)):
                        product(g, "gu" + k, 2 * c + up, [(w[:, kc, P * c:P * (c + 1)], part[g.f][:, kc, :])
                                                          for part in (XH, XL) for kc in range(KD)])

            def in_proj(g, z):
                if not z:
                    split_ready(g, "Bnext", back=1)
                for m in range(IC):
                    col = slice(INNER * z + P * m, INNER * z + P * (m + 1))
                    product(g, "izB" if z else "ixB", m,
                            [(w[:, kc, col], part[g.b][:, kc, :])
                             for w, part in ((WIH, XH), (WIL, XH), (WIH, XL)) for kc in range(KD)])

            def x_proj(g):
                pe.wait_ge(conv_step, TAPS * IC * g.index(1))
                for n, w in enumerate((WXB, WXD)):
                    product(g, "xpB", n, [(w[:, m, :], XC[g.b][:, m, :]) for m in range(IC)])

            def c_proj(g):
                pe.wait_ge(hs_ready, g.index(1))
                for m in range(IC):
                    product(g, "cpB", m, [(WC[:, P * m:P * (m + 1)], HS[g.b][:, :])])

            def onto_tokens(g, k, j, terms):
                wait(pe, res_done, 2 * g.number("token", k) + j - 1)
                for b in range(2):
                    tok = slice(P * (2 * j + b), P * (2 * j + b + 1))
                    for n, (a, c, w) in enumerate(terms):
                        ins = pe.matmul(dp[j][:, D * b:D * (b + 1)], a[:, c, tok], w[:, c, :],
                                        start=(n == 0), stop=(n == len(terms) - 1))
                ins.then_inc(d_full[j], 1)

            def down(g, k):
                pe.wait_ge(hh_ready, HC * g.number("ffn", k, 1))
                pe.wait_ge(hl_ready, HC * g.number("ffn", k, 1))
                for j in range(2):
                    onto_tokens(g, k, j, [(a[g.f], c, WD) for a in (HH, HL) for c in range(HC)])

            def out_proj(g, j):
                pe.wait_ge(yu_ready, IC * g.index(1))
                onto_tokens(g, "B", j, [(YU[g.b], m, WO) for m in range(IC)])

            def half(g):
                for what, part in tensor_order(g.h):
                    if what == "turn":
                        turn_norm(g, part)
                    elif what == "gu":
                        gate_up(g, part)
                    elif what == "down":
                        down(g, part)
                    elif what == "ix":
                        in_proj(g, 0)
                    elif what == "iz":
                        in_proj(g, 1)
                    elif what == "xp":
                        x_proj(g)
                    elif what == "cp":
                        c_proj(g)
                    else:
                        out_proj(g, int(what[-1]))

            half(Half(-1))
            half(Half(0))
            with pe.Fori(0, LOOPS) as i:
                half(Half(1, i))
                half(Half(2, i))
            half(Half(LAST - 1))
            half(Half(LAST))


_INS = ['L0_attn_x', 'L0_attn_in_proj_w', 'L0_attn_conv_w', 'L0_attn_conv_b', 'L0_attn_x_proj_w',
        'L0_attn_dt_proj_w', 'L0_attn_dt_proj_b', 'L0_attn_A_log', 'L0_attn_D', 'L0_attn_C_proj_w',
        'L0_attn_out_proj_w', 'L0_ffn_w_gate', 'L0_ffn_w_up', 'L0_ffn_w_down']
_OUTS = [((B, L, D), 'float32')]


def kernel(**inputs):
    import numpy as _np
    import concourse.bacc as _bacc
    from concourse import mybir as _mybir
    from concourse.bass_utils import run_bass_kernel_spmd as _run

    nc = _bacc.Bacc("TRN2", target_bir_lowering=False, num_devices=1)
    arrays, args = {}, []
    for name in _INS:
        a = _np.ascontiguousarray(inputs[name])
        arrays[f"in_{name}_dram"] = a
        args.append(nc.dram_tensor(f"in_{name}_dram", a.shape, _mybir.dt.from_np(a.dtype), kind="ExternalInput").ap())
    for i, (shape, dtype) in enumerate(_OUTS):
        dt = _mybir.dt.from_np(_np.dtype(dtype))
        args.append(nc.dram_tensor(f"out_{i}_dram", shape, dt, kind="ExternalOutput").ap())
    macaron(nc, *args)
    r = _run(nc, [arrays], core_ids=[0])
    got = tuple(r.results[0][f"out_{i}_dram"] for i in range(len(_OUTS)))
    return got[0]
```

```python
from contextlib import ExitStack

import concourse.bass as bass
from concourse import mybir

P = 128
B, L, D = 2, 2048, 256
TILE = 512
NB = TILE // P
STEPS = L // TILE
KD = D // P
HID = 768
HC = HID // P
INNER = 512
IC = INNER // P
N = 128
RANK = 16
TAPS = 4
EPS = 1e-5
QUANT = 1.0 / 127.0
XS = 256.0
SMALL = 0.0625

F32, F16, BF16, I32 = mybir.dt.float32, mybir.dt.float16, mybir.dt.bfloat16, mybir.dt.int32
U32 = mybir.dt.uint32
ALU = mybir.AluOpType
ACT = mybir.ActivationFunctionType
AX = mybir.AxisListType

RING = 4
SSM_STEPS = 8

LAST = 2 * STEPS
LOOPS = STEPS - 1


def has(part, h):
    return {"A": -1 <= h <= LAST - 2, "B": 0 <= h <= LAST - 1, "C": 1 <= h <= LAST}[part]


def tensor_order(h):
    if h == -1:
        return [("fill", "early", -1), ("turn", "A", -1), ("fill", "up", -1), ("gu0", "A", -1),
                ("gu1", "A", -1), ("turn", "A", 0), ("gu2", "A", -1), ("fill", "down", -1),
                ("fill", "in", -1), ("fill", "delta", -1), ("down", "A", -1), ("fill", "late", -1),
                ("gu0", "A", 0), ("turn", "Bnext", -1)]
    if h == 0:
        steps = [("ix", "B"), ("iz", "B"), ("gu1", "A"), ("xp", "B"), ("gu2", "A"), ("cp", "B"), ("down", "A")]
    else:
        steps = [("ix", "B"), ("turn", "C"), ("iz", "B"), ("gu0", "C"), ("gu1", "C"), ("gu2", "C"),
                 ("xp", "B"), ("turn", "A"), ("down", "C"), ("gu0", "A"), ("gu1", "A"), ("gu2", "A"),
                 ("cp", "B"), ("down", "A")]
    steps += [("out0", "B"), ("out1", "B"), ("turn", "Bnext"), ("out2", "B")]
    return [(what, part, h) for what, part in steps if has("A" if part == "Bnext" else part, h)]


PARTS = [(w, j) for w in "gud" for j in range(HC // 2)]
FILLS = {"early": [(w, j) for j in range(HC // 2 - 1) for w in "gu"],
         "up": [(w, HC // 2 - 1) for w in "gu"],
         "down": [("d", j) for j in range(HC // 2)],
         "in": [("i", j) for j in (0, 2, 1, 3)],
         "delta": [("dt", 0)],
         "late": [("x", 0), ("c", 0), ("o", 0), ("o", 1), ("t", 0)]}


def plan():
    number, reader, count = {}, {}, dict.fromkeys(("turn", "ffn", "token", "ring", "w_dve", "w_act"), 0)

    def take(family, part, h, n=1):
        number[family, part, h] = count[family]
        count[family] += n
        return number[family, part, h]

    for what, part, h in (step for at in range(-1, LAST + 1) for step in tensor_order(at)):
        if what == "turn":
            take("turn", part, h)
        elif what in ("down", "out0"):
            take("token", part, h)
        elif what == "fill":
            at = take("ring", part, h, len(FILLS[part]))
            for n, (w, _) in enumerate(FILLS[part]):
                last = "w_dve" if w in "ixt" else "w_act"
                count[last] += 1
                reader[at + n] = (last, count[last])
        elif what[:2] == "gu":
            if what == "gu0":
                take("ffn", part, h)
            at = take("ring", what + part, h, 4)
            for n in range(4):
                reader[at + n] = ("h" if n % 2 else "sg",
                                  HC * number["ffn", part, h] + 2 * int(what[2]) + n // 2 + 1)
        elif what == "xp":
            at = take("ring", "xpB", h, 2)
            reader[at], reader[at + 1] = ("pc", h + 1), ("bm", h + 1)
        elif what in ("ix", "iz", "cp"):
            at = take("ring", what + part, h, IC)
            for n in range(IC):
                reader[at + n] = (what, IC * h + n + 1)
    return number, reader


NUMBER, READER = plan()
PER_LOOP = {family: NUMBER[family, part, 3] - NUMBER[family, part, 1]
            for family, part in (("turn", "C"), ("ffn", "C"), ("token", "C"), ("ring", "ixB"))}
PER_LOOP |= {"sg": HC * PER_LOOP["ffn"], "h": HC * PER_LOOP["ffn"], "bm": 2, "pc": 2,
             "ix": 2 * IC, "iz": 2 * IC, "cp": 2 * IC, "half": 2, "w_dve": 0, "w_act": 0}
assert PER_LOOP["ring"] % RING == 0


class Half:

    def __init__(self, h, i=0):
        self.h, self.i = h, i
        self.b, self.f = h % 2, 1 - h % 2

    def has(self, part):
        return has(part, self.h)

    def at(self, first, family):
        return first + PER_LOOP[family] * self.i

    def number(self, family, part, more=0, back=0):
        return self.at(NUMBER[family, part, self.h - back] + more, family)

    def index(self, more=0):
        return self.at(self.h + more, "half")

    def tile(self, part):
        return (self.h + 1) // 2 - (part == "C") + self.i

    def chunk(self, part, c, up=0):
        return f"gu{c // 2}{part}", 2 * (c % 2) + up

    def bank(self, key, n):
        at = NUMBER["ring", key, self.h] + n
        return at % RING, at // RING + 1 + PER_LOOP["ring"] // RING * self.i

    def before(self, key, n):
        at = NUMBER["ring", key, self.h] + n - RING
        if at < 0:
            return None, 0
        who, count = READER[at]
        return who, self.at(count, who)


def wait(eng, sem, value):
    if not isinstance(value, int) or value > 0:
        eng.wait_ge(sem, value)


def macaron(nc, x, in_w, conv_w, conv_b, xp_w, dt_w, dt_b, a_log, d_skip, c_w, out_w, wg, wu, wd, out):
    with ExitStack() as ctx:
        def sb(name, shape, dt=F32):
            return ctx.enter_context(nc.sbuf_tensor(name, shape, dt))

        def psum(name):
            return ctx.enter_context(nc.psum_tensor(name, [P, 512], F32))

        def sem(name):
            return ctx.enter_context(nc.semaphore(name))

        S2 = range(B)
        X = [sb(f"x{s}", [P, NB, D]) for s in S2]
        XPRE = [sb(f"xpre{s}", [P, NB, D]) for s in S2]
        XH = [sb(f"xh{s}", [P, KD, TILE], F16) for s in S2]
        XL = [sb(f"xl{s}", [P, KD, TILE], F16) for s in S2]
        HH = [sb(f"hh{s}", [P, HC, TILE], F16) for s in S2]
        HL = [sb(f"hl{s}", [P, HC, TILE], F16) for s in S2]
        XI = [sb(f"xi{s}", [P, IC, TILE + 4]) for s in S2]
        XC = [sb(f"xc{s}", [P, IC, TILE]) for s in S2]
        SZ = [sb(f"sz{s}", [P, IC, TILE]) for s in S2]
        YU = [sb(f"yu{s}", [P, IC, TILE]) for s in S2]
        HS = [sb(f"hs{s}", [P, TILE]) for s in S2]
        CARRY = sb("carry", [P, B])
        XN = sb("xn", [P, NB, D])
        XCH = sb("xch", [P, IC, TILE], F16)
        XCL = sb("xcl", [P, IC, TILE], F16)
        SG = sb("sg", [P, 2, TILE])
        H = sb("h", [P, 3, TILE])
        SP = sb("sp", [P, TILE])
        DL = sb("dl", [P, TILE])
        DA = sb("da", [P, TILE])
        EX = sb("ex", [P, TILE])
        BM = sb("bm", [P, TILE])
        SER = sb("ser", [P, TILE])
        AB = sb("ab", [P, TILE])
        BB = sb("bb", [P, TILE])
        ST, MV, MN, VO, VI, VE, RS = ({k: sb(f"{name}_{k}", [P, NB, *w]) for k in ("A", "Bnext", "C")}
                                      for name, w in (("st", [6]), ("mv", [3]), ("mn", []), ("vo", []),
                                                      ("vi", []), ("ve", []), ("rs", [])))
        NEGH = sb("negh", [P, NB])
        IDN = sb("idn", [P, P])
        WG2, WG3, WU2, WU3 = (sb(n, [P, KD, HID], BF16) for n in ("wg2", "wg3", "wu2", "wu3"))
        WD2, WD3 = (sb(n, [P, HC, D], BF16) for n in ("wd2", "wd3"))
        WG = sb("wg", [P, KD, HID], BF16)
        WU = sb("wu", [P, KD, HID], BF16)
        WD = sb("wd", [P, HC, D], BF16)
        WIH = sb("wih", [P, KD, 2 * INNER], F16)
        WIL = sb("wil", [P, KD, 2 * INNER], F16)
        WXH = [sb(f"wxh{n}", [P, IC, N], F16) for n in range(2)]
        WXL = [sb(f"wxl{n}", [P, IC, N], F16) for n in range(2)]
        WC = sb("wc", [P, INNER])
        WO = sb("wo", [P, IC, D])
        CW = sb("cw", [P, IC, TAPS])
        CB = sb("cb", [P, IC])
        DS = sb("ds", [P, IC])
        DTB = sb("dtb", [P, 1])
        AL = sb("al", [P, 1])
        A = sb("a", [P, 1])
        NM = sb("nm", [P, 1], I32)
        IA = sb("ia", [P, 1])
        ONE = sb("one", [P, 1])
        SPARE = sb("spare", [1, 5])
        NSM = sb("nsm", [P, 1])
        NA = sb("na", [P, 1])
        WMX = sb("wmx", [P, 2 * HC + KD])
        GUD = slice(0, 2 * HC), slice(2 * HC, 2 * HC + KD)
        OVER = sb("over", [P, 2 * HC + KD])
        FLAG = sb("flag", [1, 2], I32)
        ER = sb("er", [P, 1])
        EK = sb("ek", [P, 1])
        EY = sb("ey", [P, 1])
        E2 = sb("e2", [P, 1], I32)
        HSC = sb("hsc", [P, HC])
        HSM = sb("hsm", [P, HC])
        HSI = sb("hsi", [P, HC])
        RMX = sb("rmx", [P, 2 * IC])
        RSC = sb("rsc", [P, 2 * IC])
        RIV = sb("riv", [P, 2 * IC])
        XSC = sb("xsc", [P, 1])
        CBA = sb("cba", [P, IC])
        XCB = sb("xcb", [P, IC])
        XM = sb("xm", [P, 1])
        XMB = sb("xmb", [P, P])
        XRM = sb("xrm", [P, 2])
        XRS = sb("xrs", [P, 2])
        XRI = sb("xri", [P, 2])
        DTN = sb("dtn", [P, RANK])
        XPD = sb("xpd", [RANK, INNER])
        DTT = sb("dtt", [RANK, N])
        NGI = HH[0][:, :, :].bitcast(I32).rearrange("p c (u f) -> p (c u) f", f=D)
        NUI = HL[0][:, :, :].bitcast(I32).rearrange("p c (u f) -> p (c u) f", f=D)
        NDI = HH[1][:, :, :].bitcast(I32).rearrange("p c t -> p (c t)").rearrange("p (a h) -> p a h", h=HID)
        NG = SZ[0][:, 0:3, :].rearrange("p c (u f) -> p (c u) f", f=D)
        NU = SZ[1][:, 0:3, :].rearrange("p c (u f) -> p (c u) f", f=D)
        ND = YU[0][:, 0:3, :].rearrange("p c t -> p (c t)").rearrange("p (a h) -> p a h", h=HID)
        NI = XC[0][:, :, :].rearrange("p c (u f) -> p (c u) f", f=D)
        NIS = XC[1][:, :, :].rearrange("p c (u f) -> p (c u) f", f=D)
        NX = YU[1][:, 0, :]
        NXS = YU[0][:, 3, :]
        NTS = SZ[0][:, 3, :]
        NC = YU[1][:, 1, :].rearrange("p (m n) -> p m n", n=N)
        NO = YU[1][:, 2:4, :]

        q = [psum(f"q{j}") for j in range(RING)]
        tp = [psum(f"tp{j}") for j in range(KD)]
        dp = [psum(f"dp{j}") for j in range(2)]

        ld_x = [sem(f"ld_x{s}") for s in S2]
        ld = {n: sem("ld_" + n) for n in ("d", "i", "x", "c", "o", "dt", "small")}
        ld_g, ld_u = ([sem(f"ld_{w}{j}") for j in range(HC // 2)] for w in "gu")
        st_y = [sem(f"st_y{s}") for s in S2]
        idn_zero, idn_ready = sem("idn_zero"), sem("idn_ready")
        cast_g, cast_u, cast_d = sem("cast_g"), sem("cast_u"), sem("cast_d")
        wmx_ready, over_ready, over_full, flag_ready = (
            sem(n) for n in ("wmx_ready", "over_ready", "over_full", "flag_ready"))
        w_dve, w_act = sem("w_dve"), sem("w_act")
        parts_full, parts_read, parts_step = sem("parts_full"), sem("parts_read"), sem("parts_step")
        rows_ready, in_scaled = sem("rows_ready"), sem("in_scaled")
        w_hi = sem("w_hi")
        xm_ready, xm_full, xrow_ready, x_scaled, unscale_ready = (
            sem(n) for n in ("xm_ready", "xm_full", "xrow_ready", "x_scaled", "unscale_ready"))
        dt_turned = sem("dt_turned")
        dtt_ready = sem("dtt_ready")
        small = sem("small")
        const_ready = sem("const_ready")
        zeroed = sem("zeroed")
        res_done = sem("res_done")
        ln_step, rs_ready = sem("ln_step"), sem("rs_ready")
        negh_ready = sem("negh_ready")
        xn_ready = sem("xn_ready")
        t_full = [sem(f"t_full{j}") for j in range(KD)]
        t_hi = [sem(f"t_hi{j}") for j in range(KD)]
        t_lo = [sem(f"t_lo{j}") for j in range(KD)]
        q_full = [sem(f"q_full{j}") for j in range(RING)]
        d_full = [sem(f"d_full{j}") for j in range(2)]
        sg_ready, h_ready, hh_ready, hl_ready = sem("sg_ready"), sem("h_ready"), sem("hh_ready"), sem("hl_ready")
        xi_ready, xi_free, conv_step = sem("xi_ready"), sem("xi_free"), sem("conv_step")
        xch_ready, xcl_ready = sem("xch_ready"), sem("xcl_ready")
        sz_ready, yu_half, yu_ready = sem("sz_ready"), sem("yu_half"), sem("yu_ready")
        pc_ready, ep_ready, sp_ready = sem("pc_ready"), sem("ep_ready"), sem("sp_ready")
        ex_ready, bm_ready = sem("ex_ready"), sem("bm_ready")
        ssm_step, hs_ready, carried = sem("ssm_step"), sem("hs_ready"), sem("carried")

        def xrows(s, t):
            return x[s, bass.ds(t * TILE, TILE), :].rearrange("(b p) d -> p b d", p=P)

        def orows(s, t):
            return out[s, bass.ds(t * TILE, TILE), :].rearrange("(b p) d -> p b d", p=P)

        block = ctx.enter_context(nc.Block())

        @block.sync
        def _(sp):
            sp.dma_start(XPRE[0][:, :, :], xrows(0, 0)).then_inc(ld_x[0], 16)
            for j in range(HC // 2):
                sp.dma_start(NGI[:, 2 * j:2 * j + 2, :], wg[2 * P * j:2 * P * (j + 1), :]
                             .rearrange("(c p) f -> p c f", p=P)).then_inc(ld_g[j], 16)
            sp.dma_start(NDI, wd.rearrange("(a p) h -> p a h", p=P)).then_inc(ld["d"], 16)
            sp.dma_start(XPRE[1][:, :, :], xrows(1, 0)).then_inc(ld_x[1], 16)
            sp.dma_start(NI, in_w.rearrange("(c p) f -> p c f", p=P)).then_inc(ld["i"], 16)
            sp.dma_start(NX, xp_w[RANK:RANK + N, :]).then_inc(ld["x"], 16)
            sp.dma_start(XPD[:, :], xp_w[0:RANK, :]).then_inc(ld["dt"], 16)
            sp.dma_start(DTN[:, :], dt_w).then_inc(ld["dt"], 16)
            sp.dma_start(CW[:, :, :], conv_w.rearrange("(m p) o k -> p m (o k)", p=P)).then_inc(ld["small"], 16)
            sp.dma_start(CB[:, :], conv_b.rearrange("(m p) -> p m", p=P), allow_slow_non_contiguous=True).then_inc(ld["small"], 16)
            sp.dma_start(DS[:, :], d_skip.rearrange("(m p) -> p m", p=P), allow_slow_non_contiguous=True).then_inc(ld["small"], 16)
            sp.dma_start(DTB[:, :], dt_b.rearrange("(p o) -> p o", o=1)).then_inc(ld["small"], 16)
            sp.dma_start(AL[:, :], a_log.rearrange("(p o) -> p o", o=1)).then_inc(ld["small"], 16)
            sp.dma_start(NC, c_w.rearrange("(m p) n -> p m n", p=P)).then_inc(ld["c"], 16)
            sp.dma_start(NO, out_w.rearrange("(a p) i -> p a i", p=P)).then_inc(ld["o"], 16)

            def half(g):
                if g.has("A") and g.h > 0:
                    sp.wait_ge(res_done, 2 * g.number("token", "A", back=2) + 2)
                    sp.dma_start(XPRE[g.f][:, :, :], xrows(g.f, g.tile("A"))).then_inc(ld_x[g.f], 16)
                if g.has("C"):
                    for j in range(2):
                        blocks = slice(2 * j, 2 * j + 2)
                        sp.wait_ge(res_done, 2 * g.number("token", "C") + j + 1)
                        sp.dma_start(orows(g.f, g.tile("C"))[:, blocks, :], X[g.f][:, blocks, :])\
                            .then_inc(st_y[g.f], 16)

            with sp.Fori(0, LOOPS) as i:
                half(Half(1, i))
                half(Half(2, i))
            half(Half(LAST - 1))
            half(Half(LAST))
            for s in S2:
                sp.wait_ge(st_y[s], 32 * STEPS)

        @block.gpsimd
        def _(pool):
            pool.memset(IDN[:, :], 0.0).then_inc(idn_zero, 1)
            pool.wait_ge(idn_zero, 1)
            pool.affine_select(out=IDN[:, :], in_=IDN[:, :], compare_op=ALU.not_equal, fill=1.0, base=0,
                               pattern=[[-1, P]], channel_multiplier=1).then_inc(idn_ready, 1)
            pool.memset(NEGH[:, :], -0.5).then_inc(negh_ready, 1)

            def root(g, k):
                pool.wait_ge(ln_step, 4 * g.number("turn", k) + 4)
                pool.tensor_tensor(RS[k][:, :], VE[k][:, :], NEGH[:, 0:NB], ALU.pow).then_inc(rs_ready, 1)

            pool.wait_ge(negh_ready, 1)
            root(Half(-1), "A")
            pool.wait_ge(ld["d"], 16)
            pool.tensor_copy(ND, NDI).then_inc(cast_d, 1)
            root(Half(0), "A")

            def hidden_low(g, k, chunks=range(HC)):
                for c in chunks:
                    pool.wait_ge(hh_ready, HC * g.number("ffn", k) + c + 1)
                    j = (HC * NUMBER["ffn", k, g.h] + c) % 3
                    pool.tensor_tensor(HL[g.f][:, c, :], H[:, j, :], HH[g.f][:, c, :], ALU.subtract)\
                        .then_inc(hl_ready, 1)

            def conv_low(g, chunks):
                for m in chunks:
                    pool.wait_ge(xch_ready, IC * g.index() + m + 1)
                    pool.tensor_tensor(XCL[:, m, :], XC[g.b][:, m, :], XCH[:, m, :], ALU.subtract)\
                        .then_inc(xcl_ready, 1)

            def gate_y(g):
                for m in range(IC):
                    pool.wait_ge(sz_ready, IC * g.index() + m + 1)
                    pool.wait_ge(yu_half, IC * g.index() + m + 1)
                    pool.tensor_tensor(YU[g.b][:, m, :], YU[g.b][:, m, :], SZ[g.b][:, m, :], ALU.mult)\
                        .then_inc(yu_ready, 1)

            def half(g):
                if g.h == 0:
                    conv_low(g, (0, 1, 2))
                    hidden_low(g, "A", (0, 1))
                    conv_low(g, (3,))
                    hidden_low(g, "A", range(2, HC))
                if g.has("C"):
                    root(g, "C")
                    if g.has("B"):
                        conv_low(g, (0, 1))
                    hidden_low(g, "C", (0,))
                    if g.has("B"):
                        conv_low(g, (2,))
                    hidden_low(g, "C", (1, 2))
                    if g.has("B"):
                        conv_low(g, (3,))
                    hidden_low(g, "C", (3,))
                if g.has("A") and g.h > 0:
                    root(g, "A")
                if g.has("C"):
                    hidden_low(g, "C", range(HC - 2, HC))
                if g.has("A") and g.h != 0:
                    hidden_low(g, "A")
                if g.has("B"):
                    gate_y(g)
                if g.has("A"):
                    root(g, "Bnext")

            half(Half(-1))
            half(Half(0))
            with pool.Fori(0, LOOPS) as i:
                half(Half(1, i))
                half(Half(2, i))
            half(Half(LAST - 1))
            half(Half(LAST))

        @block.scalar
        def _(act):
            for j in range(HC // 2):
                act.dma_start(NUI[:, 2 * j:2 * j + 2, :], wu[2 * P * j:2 * P * (j + 1), :]
                              .rearrange("(c p) f -> p c f", p=P)).then_inc(ld_u[j], 16)
            def table(func, n):
                act.activation(SPARE[:, n:n + 1], ONE[0:1, 0:1], func)

            act.wait_ge(zeroed, 2)
            table(ACT.Silu, 0)
            for j in range(HC // 2):
                for nat, ints, load, cast in ((NG, NGI, ld_g, cast_g), (NU, NUI, ld_u, cast_u)):
                    act.wait_ge(load[j], 16)
                    act.activation(nat[:, 2 * j:2 * j + 2, :], ints[:, 2 * j:2 * j + 2, :], ACT.Copy).then_inc(cast, 1)

            def filled(when, n):
                at = NUMBER["ring", when, -1] + n
                act.wait_ge(q_full[at % RING], at // RING + 1)
                return q[at % RING]

            def fills(when):
                if when == "in":
                    act.wait_ge(dt_turned, 1)
                    act.activation(DTT[:, :], tp[0][0:RANK, 0:N], ACT.Copy).then_inc(dtt_ready, 1)
                for n, (w, j) in enumerate(FILLS[when]):
                    bank = filled(when, n)
                    pair = bank[:, :].rearrange("p (k h) -> p k h", k=2)
                    if w in "gu":
                        act.activation((WG if w == "g" else WU)[:, :, 2 * P * j:2 * P * (j + 1)], pair, ACT.Copy)\
                            .then_inc(w_act, 1)
                    elif w == "d":
                        act.wait_ge(const_ready, 1)
                        act.activation(WD[:, 2 * j, :], bank[:, 0:D], ACT.Copy, scale=HSI[:, 2 * j:2 * j + 1])
                        act.activation(WD[:, 2 * j + 1, :], bank[:, D:2 * D], ACT.Copy,
                                       scale=HSI[:, 2 * j + 1:2 * j + 2]).then_inc(w_act, 1)
                    elif w == "i":
                        act.activation(WIH[:, j // 2, 512 * (j % 2):512 * (j % 2 + 1)], bank[:, :], ACT.Copy)\
                            .then_inc(w_hi, 1)
                    elif w == "dt":
                        act.wait_ge(xrow_ready, 1)
                        act.activation(NXS, NX, ACT.Copy, scale=XRS[:, 0:1]).then_inc(x_scaled, 1)
                        act.wait_ge(xrow_ready, 2)
                        act.activation(NTS, bank[:, :], ACT.Copy, scale=XRS[:, 1:2]).then_inc(w_act, 1)
                    elif w in "xt":
                        act.activation(WXH[int(w == "t")][:, :, :].rearrange("p k n -> p (k n)"), bank[:, :], ACT.Copy)\
                            .then_inc(w_hi, 1)
                    elif w == "c":
                        act.activation(WC[:, :], bank[:, :], ACT.Copy).then_inc(w_act, 1)
                    else:
                        act.activation(WO[:, 2 * j:2 * j + 2, :], pair, ACT.Copy).then_inc(w_act, 1)

            def norm_hi(g, k):
                for kc in range(KD):
                    act.wait_ge(t_full[kc], g.number("turn", k) + 1)
                    act.activation(XH[g.f][:, kc, :], tp[kc][:, :], ACT.Copy, scale=XS).then_inc(t_hi[kc], 1)

            def hidden(g, k, chunks=range(HC + 1)):
                first = HC * NUMBER["ffn", k, g.h]
                for c in chunks:
                    n = HC * g.number("ffn", k) + c
                    if c < HC:
                        bank, uses = g.bank(*g.chunk(k, c))
                        act.wait_ge(q_full[bank], uses)
                        wait(act, h_ready, n - 1)
                        act.activation(SG[:, (first + c) % 2, :], q[bank][:, :], ACT.Silu, scale=QUANT / XS)\
                            .then_inc(sg_ready, 1)
                    if c > 0:
                        act.wait_ge(h_ready, n)
                        act.activation(HH[g.f][:, c - 1, :], H[:, (first + c - 1) % 3, :], ACT.Copy)\
                            .then_inc(hh_ready, 1)

            def conv_in(g):
                wait(act, xi_free, g.index(-1))
                for m in range(IC):
                    bank, uses = g.bank("ixB", m)
                    act.wait_ge(q_full[bank], uses)
                    act.activation(XI[g.b][:, m, TAPS - 1:TAPS - 1 + TILE], q[bank][:, :], ACT.Copy,
                                   scale=RIV[:, m:m + 1]).then_inc(xi_ready, 1)

            def conv_high(g, chunks):
                for m in chunks:
                    act.wait_ge(conv_step, TAPS * (IC * g.index() + m + 1))
                    act.activation(XCH[:, m, :], XC[g.b][:, m, :], ACT.Copy).then_inc(xch_ready, 1)

            def silu_z(g):
                wait(act, yu_ready, IC * g.index(-1))
                for m in range(IC):
                    bank, uses = g.bank("izB", m)
                    act.wait_ge(q_full[bank], uses)
                    act.activation(SZ[g.b][:, m, :], q[bank][:, :], ACT.Silu,
                                   scale=RIV[:, IC + m:IC + m + 1]).then_inc(sz_ready, 1)

            def softplus(g):
                if g.h == 0:
                    act.wait_ge(unscale_ready, 1)
                table(ACT.Exp, 2)
                act.wait_ge(pc_ready, g.index(1))
                act.activation(SP[:, :], SP[:, :], ACT.Exp, scale=XRI[:, 1:2]).then_inc(ep_ready, 1)
                act.wait_ge(ep_ready, g.index(1))
                act.activation(SP[:, :], SP[:, :], ACT.Ln, bias=ONE[:, 0:1]).then_inc(sp_ready, 1)
                if g.h == 0 or not g.has("A"):
                    table(ACT.Exp, 3)

            def decay(g):
                act.wait_ge(ssm_step, SSM_STEPS * g.index() + 1)
                act.activation(EX[:, :], DL[:, :], ACT.Relu, bias=NSM[:, 0:1], scale=NA[:, 0:1])\
                    .then_inc(ex_ready, 1)
                act.wait_ge(ex_ready, 2 * g.index() + 1)
                act.activation(EX[:, :], EX[:, :], ACT.Exp, scale=-1.0).then_inc(ex_ready, 1)
                table(ACT.Silu, 4)
                bank, uses = g.bank("xpB", 1)
                act.wait_ge(q_full[bank], uses)
                act.activation(BM[:, :], q[bank][:, :], ACT.Copy, scale=IA[:, 0:1]).then_inc(bm_ready, 1)

            def half(g):
                table(ACT.Silu, 1)
                if g.has("B"):
                    conv_in(g)
                if g.has("C"):
                    norm_hi(g, "C")
                if g.has("B"):
                    silu_z(g)
                if g.has("B"):
                    conv_high(g, (0,))
                if g.h == 0:
                    conv_high(g, (1, 2))
                    hidden(g, "A", (2, 3))
                    conv_high(g, (3,))
                if g.has("C"):
                    hidden(g, "C", (0,))
                    if g.has("B"):
                        conv_high(g, (1,))
                    hidden(g, "C", (1,))
                    if g.has("B"):
                        conv_high(g, (2,))
                    hidden(g, "C", (2, 3))
                    if g.has("B"):
                        conv_high(g, (3,))
                    hidden(g, "C", (4, 5, 6))
                if g.has("B"):
                    softplus(g)
                if g.has("A") and g.h > 0:
                    norm_hi(g, "A")
                if g.h == 0:
                    act.wait_ge(const_ready, 2)
                if g.has("B"):
                    decay(g)
                if g.h == 0:
                    hidden(g, "A", range(4, HC + 1))
                if g.has("A") and g.h > 0:
                    hidden(g, "A")
                if g.has("A"):
                    norm_hi(g, "Bnext")

            fills("early")
            def scale_rows(blocks):
                act.wait_ge(rows_ready, 1)
                for c in blocks:
                    act.activation(NIS[:, c, :], NI[:, c, :], ACT.Copy, scale=RSC[:, c:c + 1]).then_inc(in_scaled, 1)

            norm_hi(Half(-1), "A")
            fills("up")
            hidden(Half(-1), "A", (0, 1, 2, 3))
            norm_hi(Half(0), "A")
            scale_rows(range(2))
            hidden(Half(-1), "A", (4,))
            scale_rows(range(2, 4))
            hidden(Half(-1), "A", (5,))
            scale_rows(range(4, 8))
            hidden(Half(-1), "A", (6,))
            fills("down")
            fills("in")
            fills("delta")
            fills("late")
            hidden(Half(0), "A", (0, 1))
            act.wait_ge(zeroed, 2)
            norm_hi(Half(-1), "Bnext")
            half(Half(0))
            with act.Fori(0, LOOPS) as i:
                half(Half(1, i))
                half(Half(2, i))
            half(Half(LAST - 1))
            half(Half(LAST))

        @block.vector
        def _(dve):
            dve.memset(CARRY[:, :], 0.0).then_inc(zeroed, 1)
            dve.memset(NSM[:, :], -SMALL)
            dve.memset(ONE[:, :], 1.0).then_inc(zeroed, 1)

            def stats(g, k, blocks):
                if k == "A":
                    dve.wait_ge(ld_x[g.f], 16 * g.tile("A") + 16)
                else:
                    before = g.number("token", "A") if k == "Bnext" else g.number("token", "B", back=1)
                    dve.wait_ge(res_done, 2 * before + 1 + (blocks[0] > 0))
                src = XPRE[g.f] if k == "A" else X[g.f]
                for b in blocks:
                    ins = dve.bn_stats(ST[k][:, b, :], src[:, b, :])
                if blocks[-1] == NB - 1:
                    ins.then_inc(ln_step, 1)

            def variance(g, k):
                at = 4 * g.number("turn", k)
                dve.wait_ge(ln_step, at + 1)
                dve.tensor_tensor(MV[k][:, :, 0], ST[k][:, :, 1], ST[k][:, :, 4], ALU.add)
                dve.tensor_tensor(MV[k][:, :, 1], ST[k][:, :, 1], ST[k][:, :, 4], ALU.subtract)
                dve.tensor_tensor(MV[k][:, :, 2], ST[k][:, :, 2], ST[k][:, :, 5], ALU.add).then_inc(ln_step, 1)
                dve.wait_ge(ln_step, at + 2)
                dve.tensor_scalar(MN[k][:, :], MV[k][:, :, 0], 0.5, None, ALU.mult)
                dve.scalar_tensor_tensor(out=VO[k][:, :], in0=MV[k][:, :, 1], scalar=0.25, in1=MV[k][:, :, 1],
                                         op0=ALU.mult, op1=ALU.mult)
                dve.tensor_scalar(VI[k][:, :], MV[k][:, :, 2], 1.0 / D, EPS, ALU.mult, ALU.add)\
                    .then_inc(ln_step, 1)
                dve.wait_ge(ln_step, at + 3)
                dve.tensor_tensor(VE[k][:, :], VO[k][:, :], VI[k][:, :], ALU.add).then_inc(ln_step, 1)

            def normalize(g, k):
                src = XPRE[g.f] if k == "A" else X[g.f]
                dve.wait_ge(rs_ready, g.number("turn", k, 1))
                for b in range(NB):
                    ins = dve.tensor_scalar(XN[:, b, :], src[:, b, :], MN[k][:, b:b + 1],
                                            RS[k][:, b:b + 1], ALU.subtract, ALU.mult)
                    if b % 2:
                        ins.then_inc(xn_ready, 1)

            def norm_lo(g, k):
                for kc in range(KD):
                    dve.wait_ge(t_hi[kc], g.number("turn", k, 1))
                    dve.scalar_tensor_tensor(out=XL[g.f][:, kc, :], in0=tp[kc][:, :], scalar=XS,
                                             in1=XH[g.f][:, kc, :], op0=ALU.mult, op1=ALU.subtract)\
                        .then_inc(t_lo[kc], 1)

            def hidden(g, k, chunks):
                for c in chunks:
                    n = HC * g.number("ffn", k) + c
                    first = HC * NUMBER["ffn", k, g.h] + c
                    bank, uses = g.bank(*g.chunk(k, c, 1))
                    dve.wait_ge(q_full[bank], uses)
                    dve.wait_ge(sg_ready, n + 1)
                    wait(dve, hl_ready, n - 2)
                    dve.scalar_tensor_tensor(out=H[:, first % 3, :], in0=SG[:, first % 2, :],
                                             scalar=HSM[:, c:c + 1], in1=q[bank][:, :],
                                             op0=ALU.mult, op1=ALU.mult).then_inc(h_ready, 1)

            def residual(g, k, j, back=0):
                s = g.b if k == "B" else g.f
                if back:
                    s = g.f
                if k == "A":
                    wait(dve, st_y[s], 32 * g.tile("A"))
                dve.wait_ge(d_full[j], g.number("token", k, 1, back))
                src = XPRE[s] if k == "A" else X[s]
                dve.scalar_tensor_tensor(
                    out=X[s][:, 2 * j:2 * j + 2, :], in0=dp[j][:, :].rearrange("p (b d) -> p b d", d=D),
                    scalar=1.0 if k == "B" else 0.5 * QUANT, in1=src[:, 2 * j:2 * j + 2, :],
                    op0=ALU.mult, op1=ALU.add).then_inc(res_done, 1)

            def conv(g, m, taps):
                s = g.b
                for k in taps:
                    if k == TAPS - 1:
                        dve.wait_ge(xi_ready, IC * g.index() + m + 1)
                        dve.tensor_scalar(XC[s][:, m, :], XI[s][:, m, k:k + TILE], CW[:, m, k:k + 1],
                                          CB[:, m:m + 1], ALU.mult, ALU.add).then_inc(conv_step, 1)
                    else:
                        dve.wait_ge(conv_step, TAPS * (IC * g.index() + m) + TAPS - 1 - k)
                        dve.scalar_tensor_tensor(out=XC[s][:, m, :], in0=XI[s][:, m, k:k + TILE],
                                                 scalar=CW[:, m, k:k + 1], in1=XC[s][:, m, :],
                                                 op0=ALU.mult, op1=ALU.add).then_inc(conv_step, 1)
                if m == IC - 1 and taps[-1] == 0:
                    dve.wait_ge(conv_step, TAPS * IC * g.index(1))
                    dve.tensor_copy(XI[s][:, :, 0:TAPS - 1], XI[s][:, :, TILE:TILE + TAPS - 1])\
                        .then_inc(xi_free, 1)

            def delta_in(g):
                bank, uses = g.bank("xpB", 0)
                dve.wait_ge(q_full[bank], uses)
                dve.tensor_scalar(SP[:, :], q[bank][:, :], DTB[:, 0:1], 0.0, ALU.add, ALU.min)\
                    .then_inc(pc_ready, 1)

            def delta(g):
                dve.wait_ge(sp_ready, g.index(1))
                dve.tensor_scalar(DL[:, :], SP[:, :], 0.001, 0.1, ALU.max, ALU.min).then_inc(ssm_step, 1)
                dve.wait_ge(ssm_step, SSM_STEPS * g.index() + 1)
                dve.tensor_scalar(DA[:, :], DL[:, :], A[:, 0:1], -SMALL, ALU.mult, ALU.max).then_inc(ssm_step, 1)

            def series(g):
                at = SSM_STEPS * g.index()
                dve.wait_ge(ssm_step, at + 2)
                dve.scalar_tensor_tensor(out=SER[:, :], in0=DA[:, :], scalar=4.0, in1=DA[:, :],
                                         op0=ALU.add, op1=ALU.mult).then_inc(ssm_step, 1)
                dve.wait_ge(ssm_step, at + 3)
                dve.scalar_tensor_tensor(out=SER[:, :], in0=SER[:, :], scalar=12.0, in1=DA[:, :],
                                         op0=ALU.add, op1=ALU.mult).then_inc(ssm_step, 1)
                dve.wait_ge(ssm_step, at + 4)
                dve.scalar_tensor_tensor(out=SER[:, :], in0=SER[:, :], scalar=24.0, in1=DA[:, :],
                                         op0=ALU.add, op1=ALU.mult).then_inc(ssm_step, 1)
                dve.wait_ge(ssm_step, at + 5)
                dve.tensor_scalar(SER[:, :], SER[:, :], 1.0 / 24.0, 1.0, ALU.mult, ALU.add).then_inc(ssm_step, 1)

            def coefficients(g):
                at = SSM_STEPS * g.index()
                dve.wait_ge(ssm_step, at + 6)
                dve.wait_ge(ex_ready, 2 * g.index(1))
                dve.tensor_tensor(AB[:, :], SER[:, :], EX[:, :], ALU.mult).then_inc(ssm_step, 1)
                dve.wait_ge(ssm_step, at + 7)
                dve.wait_ge(bm_ready, g.index(1))
                dve.scalar_tensor_tensor(out=BB[:, :], in0=AB[:, :], scalar=-1.0, in1=BM[:, :],
                                         op0=ALU.add, op1=ALU.mult).then_inc(ssm_step, 1)

            def scan(g):
                s = g.b
                dve.wait_ge(ssm_step, SSM_STEPS * g.index(1))
                wait(dve, carried, g.index())
                dve.tensor_tensor_scan(HS[s][:, :], AB[:, :], BB[:, :], CARRY[:, s:s + 1],
                                       ALU.mult, ALU.add).then_inc(hs_ready, 1)
                dve.wait_ge(hs_ready, g.index(1))
                dve.tensor_copy(CARRY[:, s:s + 1], HS[s][:, TILE - 1:TILE]).then_inc(carried, 1)

            def skip_y(g):
                for m in range(IC):
                    bank, uses = g.bank("cpB", m)
                    dve.wait_ge(q_full[bank], uses)
                    dve.scalar_tensor_tensor(out=YU[g.b][:, m, :], in0=XC[g.b][:, m, :], scalar=DS[:, m:m + 1],
                                             in1=q[bank][:, :], op0=ALU.mult, op1=ALU.add)\
                        .then_inc(yu_half, 1)

            step = [0]

            def chain(ins):
                step[0] += 1
                ins.then_inc(small, 1)
                dve.wait_ge(small, step[0])

            def power_of_two(tile):
                chain(dve.tensor_scalar(tile.bitcast(U32), tile.bitcast(U32), 0x7F800000, None, ALU.bitwise_and))

            def over(n):
                dve.wait_ge(wmx_ready, n + 1)
                dve.tensor_scalar(OVER[:, GUD[n]], WMX[:, GUD[n]], 256.0, None, ALU.is_gt).then_inc(over_ready, 1)

            def weight_flag(n):
                dve.wait_ge(over_full, n + 1)
                dve.tensor_scalar(OVER[0:1, GUD[n]], dp[0][0:1, GUD[n]], 0.0, None, ALU.add).then_inc(over_ready, 1)
                dve.wait_ge(over_ready, 2 * n + 2)
                with nc.allow_low_precision("a count"):
                    dve.tensor_reduce(FLAG[:, n:n + 1], OVER[0:1, GUD[n]], AX.X, ALU.add).then_inc(flag_ready, 1)

            def flag_value(n):
                dve.wait_ge(flag_ready, n + 1)
                return dve.value_load(FLAG[0:1, n:n + 1], min_val=0, max_val=2 ** 20)

            def hidden_scales():
                chain(dve.tensor_tensor(HSC[:, :], WMX[:, 0:HC], WMX[:, HC:2 * HC], ALU.mult))
                chain(dve.tensor_scalar(HSC[:, :], HSC[:, :], 1.0, None, ALU.max))
                chain(dve.reciprocal(HSC[:, :], HSC[:, :]))
                chain(dve.tensor_scalar(HSC[:, :], HSC[:, :], 0.99 * 2.0 ** 15 / (D * QUANT) ** 2, None, ALU.mult))
                power_of_two(HSC[:, :])
                chain(dve.tensor_scalar(HSM[:, :], HSC[:, :], QUANT / XS, None, ALU.mult))
                dve.reciprocal(HSI[:, :], HSC[:, :]).then_inc(const_ready, 1)

            def row_scales():
                dve.wait_ge(ld["i"], 16)
                chain(dve.tensor_reduce(RMX[:, :], NI, AX.X, ALU.max, apply_absolute_value=True))
                chain(dve.tensor_scalar(RMX[:, :], RMX[:, :], 1e-25, None, ALU.max))
                chain(dve.reciprocal(RSC[:, :], RMX[:, :]))
                chain(dve.tensor_scalar(RSC[:, :], RSC[:, :], 512.0, None, ALU.mult))
                power_of_two(RSC[:, :])
                chain(dve.reciprocal(RIV[:, :], RSC[:, :]))
                dve.tensor_scalar(RIV[:, :], RIV[:, :], 1.0 / XS, None, ALU.mult).then_inc(rows_ready, 1)

            def decay_rate():
                dve.wait_ge(ld["small"], 80)
                chain(dve.tensor_scalar(ER[:, :], AL[:, :], 87.0, -87.0, ALU.min, ALU.max))
                chain(dve.tensor_scalar(EK[:, :], ER[:, :], 1.4426950408889634, 1.5 * 2.0 ** 23, ALU.mult, ALU.add))
                chain(dve.tensor_scalar(EK[:, :], EK[:, :], -1.5 * 2.0 ** 23, None, ALU.add))
                chain(dve.scalar_tensor_tensor(out=ER[:, :], in0=EK[:, :], scalar=-0.693359375, in1=ER[:, :],
                                               op0=ALU.mult, op1=ALU.add))
                chain(dve.scalar_tensor_tensor(out=ER[:, :], in0=EK[:, :], scalar=2.12194440e-4, in1=ER[:, :],
                                               op0=ALU.mult, op1=ALU.add))

            def decay_series():
                chain(dve.tensor_scalar(EY[:, :], ER[:, :], 1.0 / 5040, 1.0 / 720, ALU.mult, ALU.add))
                for term in (120, 24, 6, 2, 1, 1):
                    chain(dve.tensor_scalar(EY[:, :], EY[:, :], ER[:, 0:1], 1.0 / term, ALU.mult, ALU.add))

            def decay_finish():
                chain(dve.tensor_scalar(E2[:, :], EK[:, :], 2.0 ** 23, 127 * 2.0 ** 23, ALU.mult, ALU.add))
                chain(dve.tensor_tensor(NA[:, :], EY[:, :], E2[:, :].bitcast(F32), ALU.mult))
                chain(dve.tensor_scalar(A[:, :], NA[:, :], -1.0, None, ALU.mult))
                chain(dve.tensor_scalar(NM[:, :], NA[:, :], 1e-8, None, ALU.is_le))
                chain(dve.tensor_copy(IA[:, :], A[:, :]))
                dve.wait_ge(zeroed, 2)
                chain(dve.copy_predicated(IA[:, :], NM[:, :], ONE[:, :]))
                chain(dve.reciprocal(IA[:, :], IA[:, :]))
                dve.tensor_tensor(IA[:, :], IA[:, :], XRI[:, 0:1], ALU.mult).then_inc(const_ready, 1)
                dve.wait_ge(const_ready, 2)

            def in_proj_low(banks):
                for n in banks:
                    at, j = NUMBER["ring", "in", -1] + n, FILLS["in"][n][1]
                    cols = slice(512 * (j % 2), 512 * (j % 2 + 1))
                    dve.wait_ge(w_hi, n + 1)
                    dve.tensor_tensor(WIL[:, j // 2, cols], q[at % RING][:, :], WIH[:, j // 2, cols], ALU.subtract)\
                        .then_inc(w_dve, 1)

            def x_proj_low(n):
                at = NUMBER["ring", "late", -1] + FILLS["late"].index(("xt"[n], 0))
                dve.wait_ge(w_hi, IC + n + 1)
                high, low = (w[n][:, :, :].rearrange("p k n -> p (k n)") for w in (WXH, WXL))
                dve.tensor_tensor(low, q[at % RING][:, :], high, ALU.subtract).then_inc(w_dve, 1)

            def conv_bound():
                dve.wait_ge(ld["small"], 80)
                chain(dve.tensor_reduce(XCB[:, :], CW[:, :, :], AX.X, ALU.add, apply_absolute_value=True))
                chain(dve.scalar_tensor_tensor(out=XCB[:, :], in0=XCB[:, :], scalar=float(D), in1=RMX[:, 0:IC],
                                               op0=ALU.mult, op1=ALU.mult))
                chain(dve.tensor_scalar(CBA[:, :], CB[:, :], -1.0, None, ALU.mult))
                chain(dve.tensor_tensor(CBA[:, :], CBA[:, :], CB[:, :], ALU.max))
                chain(dve.tensor_tensor(XCB[:, :], XCB[:, :], CBA[:, :], ALU.add))
                chain(dve.tensor_reduce(XM[:, :], XCB[:, :], AX.X, ALU.max))
                dve.tensor_scalar(XMB[:, :], IDN[:, :], 0.0, XM[:, 0:1], ALU.mult, ALU.add).then_inc(xm_ready, 1)

            def conv_scale():
                dve.wait_ge(xm_full, 1)
                chain(dve.tensor_reduce(XSC[:, :], tp[1][:, 0:P], AX.X, ALU.max))
                chain(dve.tensor_scalar(XSC[:, :], XSC[:, :], 1e-12, None, ALU.max))
                chain(dve.reciprocal(XSC[:, :], XSC[:, :]))
                chain(dve.tensor_scalar(XSC[:, :], XSC[:, :], 0.99 * 2.0 ** 15, None, ALU.mult))
                power_of_two(XSC[:, :])
                chain(dve.reciprocal(XM[:, :], XSC[:, :]))
                dve.tensor_scalar(CW[:, :, :], CW[:, :, :], XSC[:, 0:1], None, ALU.mult)
                dve.tensor_scalar(CB[:, :], CB[:, :], XSC[:, 0:1], None, ALU.mult)
                chain(dve.tensor_scalar(DS[:, :], DS[:, :], XM[:, 0:1], None, ALU.mult))

            def x_proj_scale(n):
                if n == 0:
                    dve.wait_ge(ld["x"], 16)
                    rows = NX
                else:
                    at = NUMBER["ring", "delta", -1]
                    dve.wait_ge(q_full[at % RING], at // RING + 1)
                    rows = q[at % RING][:, :]
                at, to = (a[:, n:n + 1] for a in (XRM, XRS))
                chain(dve.tensor_reduce(at, rows, AX.X, ALU.max, apply_absolute_value=True))
                chain(dve.tensor_scalar(at, at, 1e-12, None, ALU.max))
                chain(dve.reciprocal(to, at))
                chain(dve.tensor_scalar(to, to, 512.0, None, ALU.mult))
                dve.tensor_scalar(to.bitcast(U32), to.bitcast(U32), 0x7F800000, None, ALU.bitwise_and)\
                    .then_inc(xrow_ready, 1)
                dve.wait_ge(xrow_ready, n + 1)

            def x_proj_unscale():
                for n in range(2):
                    chain(dve.tensor_tensor(XRM[:, n:n + 1], XRS[:, n:n + 1], XSC[:, :], ALU.mult))
                chain(dve.tensor_tensor(DTB[:, :], DTB[:, :], XRM[:, 1:2], ALU.mult))
                dve.reciprocal(XRI[:, :], XRM[:, :]).then_inc(unscale_ready, 1)
                dve.wait_ge(unscale_ready, 1)

            def further_parts(flag, weights):
                with dve.If(flag > 0):
                    for w, j in weights:
                        n = PARTS.index((w, j))
                        w1, w2, w3 = {"g": (WG, WG2, WG3), "u": (WU, WU2, WU3), "d": (WD, WD2, WD3)}[w]
                        dve.wait_ge(parts_full, n + 1)
                        if w == "d":
                            w1, w2, w3 = (a[:, 2 * j:2 * j + 2, :] for a in (w1, w2, w3))
                            rest = SER[:, :].rearrange("p (k h) -> p k h", k=2)
                            for c in range(2):
                                ins = dve.scalar_tensor_tensor(
                                    out=rest[:, c, :], in0=tp[1][:, D * c:D * (c + 1)],
                                    scalar=HSI[:, 2 * j + c:2 * j + c + 1], in1=w1[:, c, :],
                                    op0=ALU.mult, op1=ALU.subtract)
                        else:
                            w1, w2, w3 = (a[:, :, 2 * P * j:2 * P * (j + 1)] for a in (w1, w2, w3))
                            rest = SER[:, :].rearrange("p (k h) -> p k h", k=KD)
                            ins = dve.tensor_tensor(rest, tp[1][:, :].rearrange("p (k h) -> p k h", k=KD), w1,
                                                    ALU.subtract)
                        ins.then_inc(parts_read, 1)
                        dve.wait_ge(parts_read, n + 1)
                        dve.tensor_copy(w2, rest).then_inc(parts_step, 1)
                        dve.wait_ge(parts_step, 2 * n + 1)
                        dve.tensor_tensor(w3, rest, w2, ALU.subtract).then_inc(parts_step, 1)
                        dve.wait_ge(parts_step, 2 * n + 2)

            first, second = Half(-1), Half(0)
            stats(first, "A", range(NB))
            variance(first, "A")
            for j in range(HC // 2):
                if j == 1:
                    normalize(first, "A")
                for nat, load, rows in ((NGI, ld_g, WMX[:, 0:HC]), (NUI, ld_u, WMX[:, HC:2 * HC])):
                    dve.wait_ge(load[j], 16)
                    ins = dve.tensor_reduce(rows[:, 2 * j:2 * j + 2], nat[:, 2 * j:2 * j + 2, :], AX.X, ALU.max,
                                            apply_absolute_value=True)
            ins.then_inc(wmx_ready, 1)
            over(0)
            weight_flag(0)
            norm_lo(first, "A")
            hidden_scales()
            flag = flag_value(0)
            dve.wait_ge(w_act, HC)
            further_parts(flag, [p for p in PARTS if p[0] != "d"])
            stats(second, "A", range(NB))
            hidden(first, "A", (0,))
            variance(second, "A")
            hidden(first, "A", (1,))
            normalize(second, "A")
            hidden(first, "A", (2,))
            row_scales()
            hidden(first, "A", (3,))
            norm_lo(second, "A")
            hidden(first, "A", (4,))
            hidden(first, "A", (5,))
            conv_bound()
            dve.wait_ge(ld["d"], 16)
            dve.tensor_reduce(WMX[:, 2 * HC:], NDI, AX.X, ALU.max, apply_absolute_value=True).then_inc(wmx_ready, 1)
            over(1)
            conv_scale()
            in_proj_low((0, 1))
            weight_flag(1)
            in_proj_low((2, 3))
            x_proj_scale(0)
            x_proj_scale(1)
            flag = flag_value(1)
            dve.wait_ge(w_act, HC + HC // 2)
            further_parts(flag, [p for p in PARTS if p[0] == "d"])
            for s in S2:
                dve.memset(XI[s][:, :, 0:TAPS - 1], 0.0).then_inc(zeroed, 1)
            dve.wait_ge(zeroed, 4)
            residual(first, "A", 0)
            stats(first, "Bnext", (0, 1))
            residual(first, "A", 1)
            stats(first, "Bnext", (2, 3))
            x_proj_low(0)
            variance(first, "Bnext")
            x_proj_low(1)
            normalize(first, "Bnext")
            hidden(second, "A", (0, 1))
            norm_lo(first, "Bnext")
            x_proj_unscale()

            def half(g):
                front, rear = (0, 1), (2, 3)
                B, C, A = g.has("B"), g.has("C"), g.has("A")
                if C:
                    residual(g, "B", 1, back=1)
                    stats(g, "C", rear)
                    variance(g, "C")
                    normalize(g, "C")
                if B:
                    conv(g, 0, (3, 2, 1, 0))
                if C:
                    norm_lo(g, "C")
                if B:
                    conv(g, 1, (3, 2, 1, 0))
                    conv(g, 2, (3, 2))
                if C:
                    hidden(g, "C", (0,))
                if B:
                    conv(g, 2, (1, 0))
                if C:
                    hidden(g, "C", (1,))
                if B:
                    conv(g, 3, (3, 2))
                if C:
                    hidden(g, "C", (2,))
                if g.h == 0:
                    hidden(g, "A", (2,))
                if B:
                    conv(g, 3, (1, 0))
                if g.h == 0:
                    hidden(g, "A", (3,))
                    decay_rate()
                    decay_series()
                if C:
                    hidden(g, "C", (3,))
                if A and g.h > 0:
                    stats(g, "A", front)
                if C:
                    hidden(g, "C", (4,))
                if A and g.h > 0:
                    stats(g, "A", rear)
                    variance(g, "A")
                if C:
                    hidden(g, "C", (5,))
                if A and g.h > 0:
                    normalize(g, "A")
                if B:
                    delta_in(g)
                    if g.h == 0:
                        decay_finish()
                    delta(g)
                if A and g.h > 0:
                    norm_lo(g, "A")
                if B:
                    series(g)
                if C and (A or not B):
                    residual(g, "C", 0)
                if B:
                    coefficients(g)
                if C and not B:
                    residual(g, "C", 1)
                if A and g.h > 0:
                    hidden(g, "A", (0,))
                if B:
                    scan(g)
                if C and B and not A:
                    residual(g, "C", 0)
                if g.h == 0:
                    hidden(g, "A", (4, 5))
                if C and B:
                    residual(g, "C", 1)
                if A and g.h > 0:
                    hidden(g, "A", (1, 2, 3, 4, 5))
                if B:
                    skip_y(g)
                if A:
                    for j in range(2):
                        residual(g, "A", j)
                        stats(g, "Bnext", (front, rear)[j])
                    variance(g, "Bnext")
                    normalize(g, "Bnext")
                if B:
                    residual(g, "B", 0)
                    if has("C", g.h + 1):
                        stats_ahead(g, front)
                if A:
                    norm_lo(g, "Bnext")

            def stats_ahead(g, blocks):
                dve.wait_ge(res_done, 2 * g.number("token", "B") + 1)
                for b in blocks:
                    dve.bn_stats(ST["C"][:, b, :], X[g.b][:, b, :])

            half(Half(0))
            with dve.Fori(0, LOOPS) as i:
                half(Half(1, i))
                half(Half(2, i))
            half(Half(LAST - 1))
            half(Half(LAST))

        @block.tensor
        def _(pe):
            pe.wait_ge(idn_ready, 1)

            def turn(dst, src, ident=None):
                return pe.transpose(dst, src, IDN[:, :] if ident is None else ident)

            readers = {"sg": sg_ready, "h": h_ready, "bm": bm_ready, "pc": pc_ready, "ix": xi_ready,
                       "iz": sz_ready, "cp": yu_half, "w_act": w_act, "w_dve": w_dve}

            def turn_weights(bank, w, j):
                for n in range(4):
                    a, b = n // 2, n % 2
                    src = {"g": lambda: NG[:, 2 * j + b, P * a:P * (a + 1)],
                           "u": lambda: NU[:, 2 * j + b, P * a:P * (a + 1)],
                           "d": lambda: ND[:, b, P * (2 * j + a):P * (2 * j + a + 1)],
                           "i": lambda: NIS[:, 4 * (j % 2) + n, P * (j // 2):P * (j // 2 + 1)],
                           "x": lambda: NXS[:, P * n:P * (n + 1)],
                           "t": lambda: NTS[:, P * n:P * (n + 1)],
                           "c": lambda: NC[:, n, :],
                           "o": lambda: NO[:, b, P * (2 * j + a):P * (2 * j + a + 1)]}[w]()
                    ins = turn(bank[:, P * n:P * (n + 1)], src)
                return ins

            def fills(when):
                loaded = {"d": (cast_d, 1), "i": (in_scaled, 0), "x": (x_scaled, 1), "dt": (dtt_ready, 1),
                          "t": (w_act, HC + HC // 2 + 1), "c": (ld["c"], 16), "o": (ld["o"], 16), "g": (cast_g, 0), "u": (cast_u, 0)}
                if when == "in":
                    pe.wait_ge(ld["dt"], 32)
                    pe.wait_ge(t_lo[0], 2)
                    turn(tp[0][0:RANK, 0:N], DTN[:, :]).then_inc(dt_turned, 1)
                for n, (w, j) in enumerate(FILLS[when]):
                    ready, count = loaded[w]
                    pe.wait_ge(ready, IC * (j % 2 + 1) if w == "i" else count or j + 1)
                    at = NUMBER["ring", when, -1] + n
                    if at >= RING:
                        who, count = READER[at - RING]
                        pe.wait_ge(readers[who], count)
                    if w == "dt":
                        ins = pe.matmul(q[at % RING][:, :], DTT[:, :], XPD[:, :], start=True, stop=True)
                    else:
                        ins = turn_weights(q[at % RING], w, j)
                    ins.then_inc(q_full[at % RING], 1)

            def count_over(n):
                pe.wait_ge(over_ready, 2 * n + 1)
                pe.matmul(dp[0][0:1, GUD[n]], ONE[:, 0:1], OVER[:, GUD[n]], start=True, stop=True)\
                    .then_inc(over_full, 1)

            def flag_value(n):
                pe.wait_ge(flag_ready, n + 1)
                return pe.value_load(FLAG[0:1, n:n + 1], min_val=0, max_val=2 ** 20)

            def further_parts(flag, weights):
                pe.wait_ge(t_lo[1], 2 if weights[0][0] == "d" else 1)
                with pe.If(flag > 0):
                    for w, j in weights:
                        n = PARTS.index((w, j))
                        if n:
                            pe.wait_ge(parts_read, n)
                        turn_weights(tp[1], w, j).then_inc(parts_full, 1)
                    pe.wait_ge(parts_step, 2 * PARTS.index(weights[-1]) + 2)

            def turn_norm(g, k):
                for kc in range(KD):
                    wait(pe, t_lo[kc], g.number("turn", k))
                for b in range(NB):
                    if b % 2 == 0:
                        pe.wait_ge(xn_ready, 2 * g.number("turn", k) + b // 2 + 1)
                    for kc in range(KD):
                        ins = turn(tp[kc][:, P * b:P * (b + 1)], XN[:, b, P * kc:P * (kc + 1)])
                        if b == NB - 1:
                            ins.then_inc(t_full[kc], 1)

            def split_waits(g, k, low, back=0):
                n = g.number("turn", k, 1, back)
                return {kc: (t_hi[kc], n) for kc in range(KD)} | {low + kc: (t_lo[kc], n) for kc in range(KD)}

            def accumulate(out, terms, more=(), over=None, waits={}):
                for at, (w, a) in enumerate(terms):
                    if at in waits:
                        pe.wait_ge(*waits[at])
                    if more and at == len(terms) - 1:
                        with pe.If(over > 0):
                            for w2, a2 in more:
                                pe.matmul(out, w2, a2, start=False, stop=False)
                    ins = pe.matmul(out, w, a, start=(at == 0), stop=(at == len(terms) - 1))
                return ins

            def product(g, key, n, terms, more=(), waits={}):
                who, count = g.before(key, n)
                if who:
                    pe.wait_ge(readers[who], count)
                bank = g.bank(key, n)[0]
                accumulate(q[bank][:, :], terms, more, flag, waits).then_inc(q_full[bank], 1)

            def gate_up(g, k, chunks):
                for c in chunks:
                    for up, (w1, w2, w3) in enumerate(((WG, WG2, WG3), (WU, WU2, WU3))):
                        def terms(*pairs):
                            return [(w[:, kc, P * c:P * (c + 1)], part[g.f][:, kc, :])
                                    for w, part in pairs for kc in range(KD)]
                        product(g, *g.chunk(k, c, up), terms((w1, XH), (w1, XL)),
                                terms((w2, XH), (w3, XH), (w2, XL)),
                                waits=split_waits(g, k, KD) if c == up == 0 else {})

            def in_proj(g, z):
                for m in range(IC):
                    col = slice(INNER * z + P * m, INNER * z + P * (m + 1))
                    product(g, "izB" if z else "ixB", m,
                            [(w[:, kc, col], part[g.b][:, kc, :])
                             for w, part in ((WIH, XH), (WIL, XH), (WIH, XL)) for kc in range(KD)],
                            waits=split_waits(g, "Bnext", 2 * KD, back=1) if not z and m == 0 else {})

            def x_proj(g):
                ready = {3 * m + 2 * low: ((xch_ready, xcl_ready)[low], IC * g.index() + m + 1)
                         for m in range(IC) for low in range(2)}
                for n in range(2):
                    product(g, "xpB", n, [(w[1 - n][:, m, :], part[:, m, :]) for m in range(IC)
                                          for w, part in ((WXH, XCH), (WXL, XCH), (WXH, XCL))],
                            waits={} if n else ready)

            def c_proj(g):
                pe.wait_ge(hs_ready, g.index(1))
                for m in range(IC):
                    product(g, "cpB", m, [(WC[:, P * m:P * (m + 1)], HS[g.b][:, :])])

            def onto_tokens(g, k, j, terms, more=(), blocks=(0, 1), waits={}):
                if blocks[0] == 0:
                    wait(pe, res_done, 2 * g.number("token", k) + j - 1)
                for b in blocks:
                    tok = slice(P * (2 * j + b), P * (2 * j + b + 1))
                    ins = accumulate(dp[j][:, D * b:D * (b + 1)], *([(a[:, c, tok], w[:, c, :]) for a, c, w in some]
                                                                    for some in (terms, more)),
                                     over=flag_down, waits=waits if j == b == 0 else {})
                if blocks[-1] == 1:
                    ins.then_inc(d_full[j], 1)

            def down(g, k):
                n = HC * g.number("ffn", k)
                waits = {c: (hh_ready, n + c + 1) for c in range(HC)} | \
                    {HC + c: (hl_ready, n + c + 1) for c in range(HC)}
                for j in range(2):
                    onto_tokens(g, k, j, [(a[g.f], c, WD) for a in (HH, HL) for c in range(HC)],
                                [(a[g.f], c, w) for a, w in ((HH, WD2), (HH, WD3), (HL, WD2)) for c in range(HC)],
                                waits=waits)

            def out_proj(g, j, blocks):
                onto_tokens(g, "B", j, [(YU[g.b], m, WO) for m in range(IC)], blocks=blocks,
                            waits={m: (yu_ready, IC * g.index() + m + 1) for m in range(IC)})

            def run(steps, this):
                for what, part, h in steps:
                    g = this if h == this.h else Half(h)
                    if what == "fill":
                        fills(part)
                    elif what == "turn":
                        turn_norm(g, part)
                    elif what[:2] == "gu":
                        gate_up(g, part, (2 * int(what[2]), 2 * int(what[2]) + 1))
                    elif what == "down":
                        down(g, part)
                    elif what == "ix":
                        in_proj(g, 0)
                    elif what == "iz":
                        in_proj(g, 1)
                    elif what == "xp":
                        x_proj(g)
                    elif what == "cp":
                        c_proj(g)
                    elif what == "out0":
                        out_proj(g, 0, (0, 1))
                    else:
                        out_proj(g, 1, (int(what[-1]) - 1,))

            def half(g):
                run(tensor_order(g.h), g)

            steps, first = tensor_order(-1), Half(-1)
            products = steps.index(("gu0", "A", -1))
            rows = steps.index(("fill", "in", -1))
            delta_rows, tokens = steps.index(("fill", "delta", -1)), steps.index(("down", "A", -1))
            run(steps[:products], first)
            count_over(0)
            flag = flag_value(0)
            further_parts(flag, [p for p in PARTS if p[0] != "d"])
            run(steps[products:rows], first)
            pe.wait_ge(xm_ready, 1)
            pe.matmul(tp[1][:, 0:P], XMB[:, :], IDN[:, :], start=True, stop=True).then_inc(xm_full, 1)
            run(steps[rows:delta_rows], first)
            count_over(1)
            run(steps[delta_rows:tokens], first)
            flag_down = flag_value(1)
            further_parts(flag_down, [p for p in PARTS if p[0] == "d"])
            run(steps[tokens:], first)
            half(Half(0))
            with pe.Fori(0, LOOPS) as i:
                half(Half(1, i))
                half(Half(2, i))
            half(Half(LAST - 1))
            half(Half(LAST))


_INS = ['L0_attn_x', 'L0_attn_in_proj_w', 'L0_attn_conv_w', 'L0_attn_conv_b', 'L0_attn_x_proj_w',
        'L0_attn_dt_proj_w', 'L0_attn_dt_proj_b', 'L0_attn_A_log', 'L0_attn_D', 'L0_attn_C_proj_w',
        'L0_attn_out_proj_w', 'L0_ffn_w_gate', 'L0_ffn_w_up', 'L0_ffn_w_down']
_OUTS = [((B, L, D), 'float32')]


def kernel(**inputs):
    import numpy as _np
    import concourse.bacc as _bacc
    from concourse import mybir as _mybir
    from concourse.bass_utils import run_bass_kernel_spmd as _run

    nc = _bacc.Bacc("TRN2", target_bir_lowering=False, num_devices=1)
    arrays, args = {}, []
    for name in _INS:
        a = _np.ascontiguousarray(inputs[name])
        arrays[f"in_{name}_dram"] = a
        args.append(nc.dram_tensor(f"in_{name}_dram", a.shape, _mybir.dt.from_np(a.dtype), kind="ExternalInput").ap())
    for i, (shape, dtype) in enumerate(_OUTS):
        dt = _mybir.dt.from_np(_np.dtype(dtype))
        args.append(nc.dram_tensor(f"out_{i}_dram", shape, dt, kind="ExternalOutput").ap())
    macaron(nc, *args)
    r = _run(nc, [arrays], core_ids=[0])
    got = tuple(r.results[0][f"out_{i}_dram"] for i in range(len(_OUTS)))
    return got[0]
```
